# Optimizing a Trainium2 kernel written in Bass

```python
import numpy as np
import jax
import jax.numpy as jnp

def _softmax(x, axis=-1):
    return jax.nn.softmax(x, axis=axis)

def _gelu(x):
    return jax.nn.gelu(x, approximate=True)

def _silu(x):
    return jax.nn.silu(x)

def _sigmoid(x):
    return jax.nn.sigmoid(x)

def _layernorm(x, axis=-1, eps=1e-05):
    m = jnp.mean(x, axis=axis, keepdims=True)
    v = jnp.var(x, axis=axis, keepdims=True)
    return (x - m) / jnp.sqrt(v + eps)

def _scatter_add(tgt, idx, src, axis=0):
    return tgt.at[idx].add(src)

def _segment_sum(src, seg, n):
    return jax.ops.segment_sum(src, seg, n)
kernel_name = 'mk_flamingo_gated_d2_seqx_r4_8abd23'

def setup_inputs(seed: int=0):
    np.random.seed(seed)
    _w = jnp.asarray

    def _rec_inputs():
        import jax
        import jax.numpy as jnp
        _rk = jax.random.key(seed)
        x = 7.22e-05 + 1 * jax.random.normal(jax.random.fold_in(_rk, 1), (4, 1024, 256), jnp.float32)
        _lenS = 1024 - jax.random.randint(jax.random.fold_in(_rk, 7), (4,), 0, max(1, 1024 // 4) + 1, jnp.int32)
        _lenS2 = 77 - jax.random.randint(jax.random.fold_in(_rk, 8), (4,), 0, max(1, 77 // 4) + 1, jnp.int32)
        _ctx_1024P = jax.random.normal(jax.random.fold_in(_rk, 11), (4, 16, 256), jnp.float32)
        _ctx_1024c = jax.random.dirichlet(jax.random.fold_in(_rk, 511), 0.3 * jnp.ones((16,), jnp.float32), (4, 77))
        _ctx_1024t = jnp.einsum('bsk,bkd->bsd', _ctx_1024c, _ctx_1024P)
        _ctx_1024t = _ctx_1024t * jax.lax.rsqrt(jnp.mean(jnp.square(_ctx_1024t)) + 1e-12) * 0.953939
        ctx_1024 = 4.13588e-05 + 0.999923 * (_ctx_1024t + 0.3 * jax.random.normal(jax.random.fold_in(_rk, 611), (4, 77, 256), jnp.float32))
        _validS = jnp.arange(1024)[None, :] < _lenS[:, None]
        _validS2 = jnp.arange(77)[None, :] < _lenS2[:, None]
        _causal = jnp.tril(jnp.ones((1024, 1024), dtype=bool))
        mask_BxS2_bk0 = jnp.logical_not(jnp.broadcast_to(_validS2[:, :], (4, 77)))
        _g = jax.random.normal(jax.random.fold_in(_rk, 9001), (2, 2), jnp.float32)
        _g = jnp.sign(_g) * jnp.maximum(jnp.abs(_g), 1.0) + (_g == 0) * 1.0
        g_xattn = _g[0]
        g_ffn = _g[1]
        return (x, ctx_1024, mask_BxS2_bk0, g_xattn, g_ffn)
    x, ctx_1024, mask_BxS2_bk0, g_xattn, g_ffn = _rec_inputs()

    def _L0_xattn_setup():
        import math
        import jax, jax.numpy as jnp
        import numpy as np
        H = 16
        D_MODEL = 256
        DK = D_MODEL // H
        K_FACTOR = 2

        def _time_delay_agg_inference(v, corr):
            B, _, _, L = v.shape
            top_k = min(int(K_FACTOR * math.log(L)), L)
            mean_value = jnp.mean(corr, axis=(1, 2))
            weights, delay = jax.lax.top_k(mean_value, top_k)
            tmp_corr = jax.nn.softmax(weights, axis=-1)
            idx = (delay[:, :, None] + jnp.arange(L)) % L
            gathered = jnp.take_along_axis(v[:, None], idx[:, :, None, None, :], axis=-1)
            return jnp.einsum('bk,bkhdl->bhdl', tmp_corr, gathered)
        key = jax.random.key(seed)
        ks = jax.random.split(key, 11)
        B, L, D = (4, 512, D_MODEL)
        s = 1.0 / math.sqrt(D)
        return {'queries': jax.random.normal(ks[0], (B, L, D), jnp.float32), 'keys': jax.random.normal(ks[1], (B, L, D), jnp.float32), 'values': jax.random.normal(ks[2], (B, L, D), jnp.float32), 'Wq': jax.random.normal(ks[3], (D, H * DK), jnp.float32) * s, 'bq': jnp.zeros((H * DK,), jnp.float32), 'Wk': jax.random.normal(ks[4], (D, H * DK), jnp.float32) * s, 'bk': jnp.zeros((H * DK,), jnp.float32), 'Wv': jax.random.normal(ks[5], (D, H * DK), jnp.float32) * s, 'bv': jnp.zeros((H * DK,), jnp.float32), 'Wo': jax.random.normal(ks[6], (H * DK, D), jnp.float32) * s, 'bo': jnp.zeros((D,), jnp.float32)}
    _L0_xattn_all = _L0_xattn_setup()
    _L0_xattn_in = {k: v for k, v in _L0_xattn_all.items() if k in ('Wq', 'bq', 'Wk', 'bk', 'Wv', 'bv', 'Wo', 'bo')}
    del _L0_xattn_all

    def _L0_ffn_setup():
        import jax, jax.numpy as jnp
        import numpy as np
        B, S, H, I, SI, E, TOPK = (2, 256, 256, 128, 512, 8, 2)
        key = jax.random.key(seed)
        ks = jax.random.split(key, 8)
        w = 0.02
        return {'hidden_states': jax.random.normal(ks[0], (B, S, H), jnp.float32), 'router_weight': jax.random.normal(ks[1], (E, H), jnp.float32) * w, 'gate_up_proj': jax.random.normal(ks[2], (E, 2 * I, H), jnp.float32) * w, 'down_proj': jax.random.normal(ks[3], (E, H, I), jnp.float32) * w, 'shared_gate_w': jax.random.normal(ks[4], (SI, H), jnp.float32) * w, 'shared_up_w': jax.random.normal(ks[5], (SI, H), jnp.float32) * w, 'shared_down_w': jax.random.normal(ks[6], (H, SI), jnp.float32) * w, 'shared_expert_gate_w': jax.random.normal(ks[7], (1, H), jnp.float32) * w}
    _L0_ffn_all = _L0_ffn_setup()
    _L0_ffn_in = {k: v for k, v in _L0_ffn_all.items() if k in ('router_weight', 'gate_up_proj', 'down_proj', 'shared_gate_w', 'shared_up_w', 'shared_down_w', 'shared_expert_gate_w')}
    del _L0_ffn_all

    def _L1_xattn_setup():
        import jax, jax.numpy as jnp
        import numpy as np
        NUM_HEADS = 16
        HIDDEN = 256
        KEY_SIZE = 64
        VALUE_SIZE = 64
        B, S = (4, 512)

        def _split_heads(x, d):
            b, s, _ = x.shape
            return x.reshape(b, s, NUM_HEADS, d).transpose(0, 2, 1, 3)
        key = jax.random.key(seed)
        ks = jax.random.split(key, 7)
        xavier = lambda k, shp: jax.random.normal(k, shp, jnp.float32) * jnp.sqrt(2.0 / (shp[0] + shp[1]))
        return {'X_Q': jax.random.normal(ks[0], (B, S, HIDDEN), jnp.float32), 'X_KV': jax.random.normal(ks[1], (B, S, HIDDEN), jnp.float32), 'key_padding_mask': jax.random.randint(ks[2], (B, S), 0, 2).astype(bool), 'W_Q': xavier(ks[3], (HIDDEN, KEY_SIZE * NUM_HEADS)), 'W_K': xavier(ks[4], (HIDDEN, KEY_SIZE * NUM_HEADS)), 'W_V': xavier(ks[5], (HIDDEN, VALUE_SIZE * NUM_HEADS)), 'W_O': xavier(ks[6], (VALUE_SIZE * NUM_HEADS, HIDDEN))}
    _L1_xattn_all = _L1_xattn_setup()
    _L1_xattn_in = {k: v for k, v in _L1_xattn_all.items() if k in ('W_Q', 'W_K', 'W_V', 'W_O')}
    del _L1_xattn_all

    def _L1_ffn_setup():
        import jax, jax.numpy as jnp
        import numpy as np
        E = 32
        K = 4
        H = 256
        I = 128
        B, S = (2, 512)
        T = B * S
        C = 256
        ROUTED_SCALE = 1.0

        def _silu_and_mul(gu):
            g, u = jnp.split(gu, 2, axis=-1)
            return jax.nn.silu(g) * u
        key = jax.random.key(seed)
        ks = jax.random.split(key, 6)
        s = 0.02
        return {'hidden_states': jax.random.normal(ks[0], (B, S, H), jnp.float32), 'gate_w': jax.random.normal(ks[1], (E, H), jnp.float32) * s, 'w_gate_up': jax.random.normal(ks[2], (E, H, 2 * I), jnp.float32) * s, 'w_down': jax.random.normal(ks[3], (E, I, H), jnp.float32) * s, 'shared_w_gate_up': jax.random.normal(ks[4], (H, 2 * I), jnp.float32) * s, 'shared_w_down': jax.random.normal(ks[5], (I, H), jnp.float32) * s}
    _L1_ffn_all = _L1_ffn_setup()
    _L1_ffn_in = {k: v for k, v in _L1_ffn_all.items() if k in ('gate_w', 'w_gate_up', 'w_down', 'shared_w_gate_up', 'shared_w_down')}
    del _L1_ffn_all
    return {'x': x, 'ctx_1024': ctx_1024, 'mask_BxS2_bk0': mask_BxS2_bk0, 'g_xattn': g_xattn, 'g_ffn': g_ffn, 'L0_xattn_Wq': _L0_xattn_in['Wq'], 'L0_xattn_bq': _L0_xattn_in['bq'], 'L0_xattn_Wk': _L0_xattn_in['Wk'], 'L0_xattn_bk': _L0_xattn_in['bk'], 'L0_xattn_Wv': _L0_xattn_in['Wv'], 'L0_xattn_bv': _L0_xattn_in['bv'], 'L0_xattn_Wo': _L0_xattn_in['Wo'], 'L0_xattn_bo': _L0_xattn_in['bo'], 'L0_ffn_router_weight': _L0_ffn_in['router_weight'], 'L0_ffn_gate_up_proj': _L0_ffn_in['gate_up_proj'], 'L0_ffn_down_proj': _L0_ffn_in['down_proj'], 'L0_ffn_shared_gate_w': _L0_ffn_in['shared_gate_w'], 'L0_ffn_shared_up_w': _L0_ffn_in['shared_up_w'], 'L0_ffn_shared_down_w': _L0_ffn_in['shared_down_w'], 'L0_ffn_shared_expert_gate_w': _L0_ffn_in['shared_expert_gate_w'], 'L1_xattn_W_Q': _L1_xattn_in['W_Q'], 'L1_xattn_W_K': _L1_xattn_in['W_K'], 'L1_xattn_W_V': _L1_xattn_in['W_V'], 'L1_xattn_W_O': _L1_xattn_in['W_O'], 'L1_ffn_gate_w': _L1_ffn_in['gate_w'], 'L1_ffn_w_gate_up': _L1_ffn_in['w_gate_up'], 'L1_ffn_w_down': _L1_ffn_in['w_down'], 'L1_ffn_shared_w_gate_up': _L1_ffn_in['shared_w_gate_up'], 'L1_ffn_shared_w_down': _L1_ffn_in['shared_w_down']}

def reference(x, ctx_1024, mask_BxS2_bk0, g_xattn, g_ffn, L0_xattn_Wq, L0_xattn_bq, L0_xattn_Wk, L0_xattn_bk, L0_xattn_Wv, L0_xattn_bv, L0_xattn_Wo, L0_xattn_bo, L0_ffn_router_weight, L0_ffn_gate_up_proj, L0_ffn_down_proj, L0_ffn_shared_gate_w, L0_ffn_shared_up_w, L0_ffn_shared_down_w, L0_ffn_shared_expert_gate_w, L1_xattn_W_Q, L1_xattn_W_K, L1_xattn_W_V, L1_xattn_W_O, L1_ffn_gate_w, L1_ffn_w_gate_up, L1_ffn_w_down, L1_ffn_shared_w_gate_up, L1_ffn_shared_w_down):
    import jax
    import jax.numpy as jnp

    def _L0_xattn_ref(queries, keys, values, Wq, bq, Wk, bk, Wv, bv, Wo, bo):
        import math
        import jax, jax.numpy as jnp
        import numpy as np
        H = 16
        D_MODEL = 256
        DK = D_MODEL // H
        K_FACTOR = 2

        def _time_delay_agg_inference(v, corr):
            B, _, _, L = v.shape
            top_k = min(int(K_FACTOR * math.log(L)), L)
            mean_value = jnp.mean(corr, axis=(1, 2))
            weights, delay = jax.lax.top_k(mean_value, top_k)
            tmp_corr = jax.nn.softmax(weights, axis=-1)
            idx = (delay[:, :, None] + jnp.arange(L)) % L
            gathered = jnp.take_along_axis(v[:, None], idx[:, :, None, None, :], axis=-1)
            return jnp.einsum('bk,bkhdl->bhdl', tmp_corr, gathered)
        B, Lq, _ = queries.shape
        Lk = keys.shape[1]
        q = (queries @ Wq + bq).reshape(B, Lq, H, DK)
        k = (keys @ Wk + bk).reshape(B, Lk, H, DK)
        v = (values @ Wv + bv).reshape(B, Lk, H, DK)
        if Lq > Lk:
            pad = ((0, 0), (0, Lq - Lk), (0, 0), (0, 0))
            k = jnp.pad(k, pad)
            v = jnp.pad(v, pad)
        else:
            k = k[:, :Lq]
            v = v[:, :Lq]
        qt = jnp.transpose(q, (0, 2, 3, 1))
        kt = jnp.transpose(k, (0, 2, 3, 1))
        vt = jnp.transpose(v, (0, 2, 3, 1))
        qf = jnp.fft.rfft(qt)
        kf = jnp.fft.rfft(kt)
        c = qf.real * kf.real + 1j * -(qf.imag * kf.imag)
        corr = jnp.fft.irfft(c, n=Lq).astype(qt.dtype)
        agg = _time_delay_agg_inference(vt, corr)
        out = jnp.transpose(agg, (0, 3, 1, 2)).reshape(B, Lq, H * DK)
        return out @ Wo + bo

    def _L0_ffn_ref(hidden_states, router_weight, gate_up_proj, down_proj, shared_gate_w, shared_up_w, shared_down_w, shared_expert_gate_w):
        import jax, jax.numpy as jnp
        import numpy as np
        B, S, H, I, SI, E, TOPK = (2, 256, 256, 128, 512, 8, 2)
        b, s, h = hidden_states.shape
        x = hidden_states.reshape(-1, h)
        shared = jax.nn.silu(x @ shared_gate_w.T) * (x @ shared_up_w.T) @ shared_down_w.T
        logits = x @ router_weight.T
        probs = jax.nn.softmax(logits.astype(jnp.float32), axis=-1)
        top_v, top_i = jax.lax.top_k(probs, TOPK)
        top_v = (top_v / jnp.sum(top_v, axis=-1, keepdims=True)).astype(logits.dtype)
        cw = jnp.sum(jax.nn.one_hot(top_i, E, dtype=top_v.dtype) * top_v[..., None], axis=1)
        gu = jnp.einsum('th,eih->eti', x, gate_up_proj)
        gate, up = jnp.split(gu, 2, axis=-1)
        act = jax.nn.silu(gate) * up
        per_expert = jnp.einsum('eti,ehi->eth', act, down_proj)
        expert_out = jnp.einsum('eth,te->th', per_expert, cw)
        out = expert_out + jax.nn.sigmoid(x @ shared_expert_gate_w.T) * shared
        return out.reshape(b, s, h)

    def _L1_xattn_ref(X_Q, X_KV, key_padding_mask, W_Q, W_K, W_V, W_O):
        import jax, jax.numpy as jnp
        import numpy as np
        NUM_HEADS = 16
        HIDDEN = 256
        KEY_SIZE = 64
        VALUE_SIZE = 64
        B, S = (4, 512)

        def _split_heads(x, d):
            b, s, _ = x.shape
            return x.reshape(b, s, NUM_HEADS, d).transpose(0, 2, 1, 3)
        Q = _split_heads(X_Q @ W_Q, KEY_SIZE)
        K = _split_heads(X_KV @ W_K, KEY_SIZE)
        V = _split_heads(X_KV @ W_V, VALUE_SIZE)
        E = jnp.einsum('bhqd,bhkd->bhqk', Q, K)
        E = jnp.where(key_padding_mask[:, None, None, :], -jnp.inf, E)
        A = jax.nn.softmax(E / jnp.sqrt(jnp.float32(KEY_SIZE)), axis=-1)
        Yp = jnp.einsum('bhqk,bhkd->bhqd', A, V)
        b, h, sq, dv = Yp.shape
        Y = Yp.transpose(0, 2, 1, 3).reshape(b, sq, h * dv) @ W_O
        return Y

    def _L1_ffn_ref(hidden_states, gate_w, w_gate_up, w_down, shared_w_gate_up, shared_w_down):
        import jax, jax.numpy as jnp
        import numpy as np
        E = 32
        K = 4
        H = 256
        I = 128
        B, S = (2, 512)
        T = B * S
        C = 256
        ROUTED_SCALE = 1.0

        def _silu_and_mul(gu):
            g, u = jnp.split(gu, 2, axis=-1)
            return jax.nn.silu(g) * u
        b, s, h = hidden_states.shape
        x = hidden_states.reshape(-1, h)
        t = x.shape[0]
        logits = x @ gate_w.T
        probs = jax.nn.softmax(logits, axis=-1)
        topk_w, topk_idx = jax.lax.top_k(probs, K)
        topk_w = topk_w / jnp.sum(topk_w, axis=-1, keepdims=True)
        topk_w = topk_w * ROUTED_SCALE
        e_flat = topk_idx.reshape(-1)
        w_flat = topk_w.reshape(-1)
        t_flat = jnp.repeat(jnp.arange(t), K)
        order = jnp.argsort(e_flat)
        e_s, w_s, t_s = (e_flat[order], w_flat[order], t_flat[order])
        counts = jax.ops.segment_sum(jnp.ones_like(e_s), e_s, num_segments=E)
        starts = jnp.cumsum(counts) - counts
        pos = jnp.arange(t * K) - starts[e_s]
        slot = jnp.minimum(pos, C)
        buf = jnp.zeros((E, C + 1, h), x.dtype).at[e_s, slot].set(x[t_s])
        gu = jnp.einsum('ech,ehi->eci', buf[:, :C], w_gate_up)
        expert_out = jnp.einsum('eci,eih->ech', _silu_and_mul(gu), w_down)
        expert_out = jnp.pad(expert_out, ((0, 0), (0, 1), (0, 0)))
        gate = jnp.where(pos < C, w_s, 0.0)[:, None]
        routed = jnp.zeros_like(x).at[t_s].add(expert_out[e_s, slot] * gate)
        shared = _silu_and_mul(x @ shared_w_gate_up) @ shared_w_down
        return (routed + shared).reshape(b, s, h)
    x = x + jnp.tanh(g_xattn[0]) * _L0_xattn_ref(_layernorm(x, axis=-1), ctx_1024, ctx_1024, L0_xattn_Wq, L0_xattn_bq, L0_xattn_Wk, L0_xattn_bk, L0_xattn_Wv, L0_xattn_bv, L0_xattn_Wo, L0_xattn_bo)
    x = x + jnp.tanh(g_ffn[0]) * _L0_ffn_ref(_layernorm(x, axis=-1), L0_ffn_router_weight, L0_ffn_gate_up_proj, L0_ffn_down_proj, L0_ffn_shared_gate_w, L0_ffn_shared_up_w, L0_ffn_shared_down_w, L0_ffn_shared_expert_gate_w)
    x = x + jnp.tanh(g_xattn[1]) * _L1_xattn_ref(_layernorm(x, axis=-1), ctx_1024, mask_BxS2_bk0, L1_xattn_W_Q, L1_xattn_W_K, L1_xattn_W_V, L1_xattn_W_O)
    x = x + jnp.tanh(g_ffn[1]) * _L1_ffn_ref(_layernorm(x, axis=-1), L1_ffn_gate_w, L1_ffn_w_gate_up, L1_ffn_w_down, L1_ffn_shared_w_gate_up, L1_ffn_shared_w_down)
    return x

_drawn_inputs = setup_inputs


def setup_inputs(seed=0):
    import zlib

    import numpy as np

    out = dict(_drawn_inputs(seed))
    spreads = {'g_ffn': (-1.0, 0.6),
     'L0_xattn_bq': (0.0, 0.8),
     'L0_xattn_bk': (0.0, 0.305),
     'L0_xattn_bv': (0.0, 0.8),
     'L0_xattn_bo': (0.0, 0.1)}
    factors = {'L0_ffn_router_weight': 8.0,
     'L0_ffn_gate_up_proj': 8.0,
     'L0_ffn_down_proj': 8.0,
     'L0_ffn_shared_gate_w': 6.707,
     'L0_ffn_shared_up_w': 6.612,
     'L0_ffn_shared_down_w': 6.597,
     'L0_ffn_shared_expert_gate_w': 8.0,
     'L1_ffn_gate_w': 8.0,
     'L1_ffn_w_gate_up': 8.0,
     'L1_ffn_w_down': 8.0,
     'L1_ffn_shared_w_gate_up': 6.149,
     'L1_ffn_shared_w_down': 6.226}
    for name, (base, spread) in spreads.items():
        noise = np.random.default_rng([zlib.crc32(name.encode()), seed]).standard_normal(out[name].shape)
        drawn = base * np.exp(spread * noise) if base else spread * noise
        out[name] = jnp.asarray(drawn.astype(out[name].dtype))
    for name, factor in factors.items():
        out[name] = (out[name] * factor).astype(out[name].dtype)
    return out
```

```python
from contextlib import ExitStack

import numpy as np

import concourse.bass as bass
from concourse import mybir

ALU = mybir.AluOpType
ACT = mybir.ActivationFunctionType
AX = mybir.AxisListType
F32 = mybir.dt.float32
BF16 = mybir.dt.bfloat16
I32 = mybir.dt.int32
F32R = mybir.dt.float32r

P = 128
B, L, D = 4, 1024, 256
S = 77
T = B * L
TILES = T // P
CHUNK = 512
CT = CHUNK // P
CHUNKS = T // CHUNK
KD = D // P
BS = B * S
TOPK = 13
WROW = L + S - 1
E0, UNITS = 8, 12
R0 = E0 + 2
H1, DK = 16, 64
HS = H1 * S
EPS = 1e-5
E1, K1, CAP = 32, 4, 256
SLOTS = E1 * CAP
ROW = 260
NEG = -3.0e38
SENTINEL = 3.3e38
MASKED = -1.0e30
FAR = 1.0e6


def want(eng, sem, value):
    if isinstance(value, int) and value <= 0:
        return
    eng.wait_ge(sem, value)


def wait_apart(eng, sem, value, passed):
    if isinstance(value, int):
        want(eng, sem, value)
    else:
        eng.wait_ge(sem, value)
        eng.sem_inc(passed, 1)


class Chain:

    def __init__(self, eng, sem, passed):
        self.passed = passed
        self.eng, self.sem, self.base, self.i, self.local = eng, sem, 0, None, 0

    def enter(self, i, per):
        self.i, self.per, self.local = i, per, 0

    def leave(self, rounds):
        assert self.local == self.per, ("steps of a round", self.local)
        self.base += self.per * rounds
        self.i = None
        self.local = 0

    def __call__(self, ins):
        ins.then_inc(self.sem, 1)
        self.local += 1
        if self.i is None:
            self.base += 1
            self.local = 0
            self.eng.wait_ge(self.sem, self.base)
        else:
            wait_apart(self.eng, self.sem, self.per * self.i + (self.base + self.local), self.passed)


def build(nc, io):
    root = ExitStack()
    with root:
        def sem(name):
            return root.enter_context(nc.semaphore(name))

        def sb(name, shape, dt=F32, at=root):
            return at.enter_context(nc.sbuf_tensor(name, shape, dt))

        bank = root.enter_context(nc.psum_tensor("bank", [P, 8, 512], F32))

        x = sb("x_res", [P, TILES, D])
        ident = sb("ident", [P, P])
        gates = sb("gates", [P, 4])
        tg = sb("tanh_gates", [P, 4])
        neghalf = sb("neghalf", [P, CT])
        wgu0 = sb("wgu0", [P, KD, UNITS * 2 * P])
        wd0 = sb("wd0", [P, UNITS, D])
        wr0 = sb("wr0", [P, KD, R0])
        vwo0 = sb("vwo0", [S + 1, B, D])
        bst = sb("bst", [P, 2, CT, 6])
        mv = sb("mv", [P, 2, CT, 2])
        veps = sb("veps", [P, 2, CT])
        rstd = sb("rstd", [P, 2, CT])
        xn = sb("xn", [P, 2, CT, D])

        passed, passed_pool, passed_pe = sem("passed"), sem("passed_pool"), sem("passed_pe")
        x_in = [sem(f"x_in{c}") for c in range(CHUNKS)]
        ident_zero, ident_ready, consts_ready = sem("ident_zero"), sem("ident_ready"), sem("consts_ready")
        gates_in, tg_ready = sem("gates_in"), sem("tg_ready")
        ffn0_w_in = sem("ffn0_w_in")
        ln_bst, ln_stats, ln_veps, ln_rstd = sem("ln_bst"), sem("ln_stats"), sem("ln_veps"), sem("ln_rstd")
        ln_xn, ln_T, ln_xT = sem("ln_xn"), sem("ln_T"), sem("ln_xT")

        st_d = nc.dram_tensor("st_d", (B, S, 2 * L), F32, kind="Internal").ap()
        w_d = nc.dram_tensor("w_d", (B, WROW), F32, kind="Internal").ap()
        wqk_d = nc.dram_tensor("wqk_d", (B, D, HS), F32, kind="Internal").ap()
        vwo_d = nc.dram_tensor("vwo_d", (B, HS, D), F32, kind="Internal").ap()
        slots_d = nc.dram_tensor("slots_d", (SLOTS, ROW), F32, kind="Internal").ap()
        y_d = nc.dram_tensor("y_d", (T * K1, D), F32, kind="Internal").ap()

        out = io["out"]
        x_v = io["x"].rearrange("(n p) d -> p n d", p=P)
        out_v = out.rearrange("(n p) d -> p n d", p=P)

        def ln_stats_job(dve, q, c, par):
            wait_apart(dve, ln_xn, 4 * (q - 1), passed)
            tile0 = c * CT
            for t in range(CT):
                dve.bn_stats(bst[:, par, t, :], x[:, bass.ds(tile0 + t, 1), :]).then_inc(ln_bst, 1)
            for t in range(CT):
                wait_apart(dve, ln_bst, 4 * q + (t + 1), passed)
                dve.bn_aggr(mv[:, par, t, :], bst[:, par, t, :]).then_inc(ln_stats, 1)

        def ln_rstd_job(pool, q, par):
            wait_apart(pool, ln_stats, 4 * q + 4, passed_pool)
            pool.tensor_scalar_add(veps[:, par, :], mv[:, par, :, 1], EPS).then_inc(ln_veps, 1)
            pool.wait_ge(ln_veps, 1 * q + 1)
            pool.tensor_tensor(rstd[:, par, :], veps[:, par, :], neghalf[:, 0:CT], ALU.pow).then_inc(ln_rstd, 1)

        def ln_norm_job(dve, q, c, par):
            dve.wait_ge(ln_rstd, q + 1)
            want(dve, ln_T, q - 1)
            tile0 = c * CT
            for t in range(CT):
                dve.tensor_scalar(xn[:, par, t, :], x[:, bass.ds(tile0 + t, 1), :], mv[:, par, t, 0:1],
                                  rstd[:, par, t:t + 1], ALU.subtract, ALU.mult).then_inc(ln_xn, 1)

        def ln_transpose_job(pe, q, par):
            pe.wait_ge(ln_xn, 4 * q + 4)
            want(pe, ln_xT, 2 * q)
            for t in range(CT):
                for k in range(KD):
                    last = pe.transpose(bank[:, k, t * P:(t + 1) * P], xn[:, par, t, k * P:(k + 1) * P], ident[:])
            last.then_inc(ln_T, 1)

        def ln_evict_job(act, q, par):
            act.wait_ge(ln_T, q + 1)
            for k in range(KD):
                act.activation(xnT[:, par, k, :], bank[:, k, :], ACT.Copy).then_inc(ln_xT, 1)

        one = ExitStack()
        with one:
            xnT = sb("xnT", [P, 2, KD, CHUNK], at=one)
            ctxT = sb("ctxT", [P, KD, BS], at=one)
            wk0 = sb("wk0", [P, KD, D], at=one)
            wqT0 = sb("wqT0", [P, KD, D], at=one)
            wv0 = sb("wv0", [P, KD, D], at=one)
            wo0 = sb("wo0", [P, KD, D], at=one)
            bias0 = sb("bias0", [P, 3, KD], at=one)
            kT0 = sb("kT0", [P, KD, BS], at=one)
            vT0 = sb("vT0", [P, KD, BS], at=one)
            wqk0 = sb("wqk0", [P, KD, BS], at=one)
            bqk = sb("bqk", [S, B], at=one)
            sT = sb("sT", [S, 2, CHUNK], at=one)
            skew = sb("skew", [S, 2, 2, L], at=one)
            signs = sb("signs", [S, 4], at=one)
            sumU = sb("sumU", [P, 8, B], at=one)
            difV = sb("difV", [P, 8, B], at=one)
            htab = sb("htab", [P, 8, CHUNK], at=one)
            urow = sb("urow", [B, L + 1], at=one)
            even = sb("even", [B, L], at=one)
            mean = sb("mean", [B, L], at=one)
            top = sb("top", [B, 16], at=one)
            left1 = sb("left1", [B, L], at=one)
            left2 = sb("left2", [B, L], at=one)
            negmax = sb("negmax", [B, 1], at=one)
            expm = urow[:, 0:L]
            wsel = even
            wsum = sb("wsum", [B, 2], at=one)
            wrow = sb("wrow", [B, WROW], at=one)
            wk1 = sb("wk1", [P, 2, KD, P], at=one)
            wv1 = sb("wv1", [P, 2, KD, P], at=one)
            wqT1 = sb("wqT1", [P, 2, D], at=one)
            wo1 = sb("wo1", [P, 2, D], at=one)
            kT1 = sb("kT1", [P, 2, BS], at=one)
            vT1 = sb("vT1", [P, 2, BS], at=one)
            wqk1 = sb("wqk1", [P, 2, KD, B, 2 * S], at=one)
            vwo1 = sb("vwo1", [S, 2, 2, B, D], at=one)

            w0_in, htab_in, bo_in = sem("w0_in"), sem("htab_in"), sem("bo_in")
            fold_mm, kT0_ready, vT0_ready = sem("fold_mm"), sem("kT0_ready"), sem("vT0_ready")
            fold_out, vwo_mm, vwo_out = sem("fold_out"), sem("vwo_mm"), sem("vwo_out")
            s_mm, s_out, s_stored = sem("s_mm"), sem("s_out"), [sem("s_stored0"), sem("s_stored1")]
            skew_in, uv_mm, uv_out = [sem("skew_in0"), sem("skew_in1")], sem("uv_mm"), sem("uv_out")
            h_mm, ex_ready, nm_ready, w_ready, w_stored = (sem("h_mm"), sem("ex_ready"), sem("nm_ready"),
                                                           sem("w_ready"), sem("w_stored"))
            w1_in = [sem("w1_in0"), sem("w1_in1")]
            kv1_mm, k1_out, v1_out = sem("kv1_mm"), sem("k1_out"), sem("v1_out")
            qk1_mm, qk1_out, vo1_mm, vo1_out = sem("qk1_mm"), sem("qk1_out"), sem("vo1_mm"), sem("vo1_out")
            qk1_stored, vo1_stored = ([sem("qk1_stored0"), sem("qk1_stored1")],
                                      [sem("vo1_stored0"), sem("vo1_stored1")])
            d1 = sem("dve_steps_1")

            with nc.Block() as block:
                @block.sync
                def _(sp):
                    for name, dst in (("ctxT", ctxT), ("wk0", wk0), ("wqT0", wqT0), ("wv0", wv0), ("wo0", wo0)):
                        sp.dma_start(dst[:], io[name].rearrange("(k p) n -> p k n", p=P)).then_inc(w0_in, 16)
                    sp.dma_start(bias0[:], io["bias0"].rearrange("p (a k) -> p a k", a=3)).then_inc(w0_in, 16)
                    for c in range(CHUNKS):
                        sp.dma_start(x[:, c * CT:(c + 1) * CT, :], x_v[:, c * CT:(c + 1) * CT, :]).then_inc(x_in[c], 16)
                    for b in range(B):
                        sp.dma_start(vwo0[S:S + 1, b, :], io["bo0"].rearrange("(a n) -> a n", a=1)).then_inc(bo_in, 16)
                    sp.dma_start(htab[:], io["htab"].rearrange("(c p) n -> p c n", p=P)).then_inc(htab_in, 16)
                    for c in range(CHUNKS):
                        b, half = c // 2, c % 2
                        sp.wait_ge(s_out, c + 1)
                        for copy in range(2):
                            sp.dma_start(st_d[b, :, copy * L + half * CHUNK:copy * L + (half + 1) * CHUNK],
                                         sT[:, half, :]).then_inc(s_stored[half], 16)
                        if half:
                            for par in range(2):
                                sp.wait_ge(s_stored[par], 32 * (b + 1))
                            want(sp, uv_mm, b - 1)
                            for sign in range(2):
                                shift = bass.AP(st_d.tensor, b * S * 2 * L + (S - 1 if sign == 0 else L - S + 1),
                                                [[2 * L - 1 if sign == 0 else 2 * L + 1, S], [1, L]])
                                sp.dma_start(skew[:, b % 2, sign, :], shift).then_inc(skew_in[b % 2], 16)
                    sp.wait_ge(w_ready, 2)
                    sp.dma_start(w_d, wrow[:]).then_inc(w_stored, 16)
                    sp.wait_ge(w_stored, 16)

                @block.gpsimd
                def _(pool):
                    pool.memset(ident[:], 0.0).then_inc(ident_zero, 1)
                    pool.memset(neghalf[:], -0.5).then_inc(consts_ready, 1)
                    pool.memset(signs[:, 0:3], 1.0).then_inc(consts_ready, 1)
                    pool.memset(signs[:, 3:4], -1.0).then_inc(consts_ready, 1)
                    pool.wait_ge(ident_zero, 1)
                    pool.affine_select(out=ident[:], in_=ident[:], compare_op=ALU.not_equal, fill=1.0, base=0,
                                       pattern=[[-1, P]], channel_multiplier=1).then_inc(ident_ready, 1)
                    pool.wait_ge(consts_ready, 3)
                    for c in range(CHUNKS):
                        ln_rstd_job(pool, c, c % 2)

                @block.scalar
                def _(act):
                    act.dma_start(gates[:, 0:2], bass.AP(io["g_xattn"].tensor, 0, [[0, P], [1, 2]])).then_inc(gates_in, 16)
                    act.dma_start(gates[:, 2:4], bass.AP(io["g_ffn"].tensor, 0, [[0, P], [1, 2]])).then_inc(gates_in, 16)
                    act.wait_ge(gates_in, 32)
                    act.activation(tg[:], gates[:], ACT.Tanh).then_inc(tg_ready, 1)

                    def load_heads(m):
                        if m >= 2:
                            act.wait_ge(vo1_mm, 8 * (m - 1))
                        cols = slice(m * P, (m + 1) * P)
                        for w, src in ((wk1, "wk1"), (wv1, "wv1")):
                            act.dma_start(w[:, m % 2, :, :], io[src].rearrange("(k p) n -> p k n", p=P)[:, :, cols])\
                               .then_inc(w1_in[m % 2], 16)
                        for w, src in ((wqT1, "wqT1"), (wo1, "wo1")):
                            act.dma_start(w[:, m % 2, :], io[src][cols, :]).then_inc(w1_in[m % 2], 16)

                    def store_heads(m):
                        act.wait_ge(qk1_out, 4 * (m + 1))
                        for b in range(B):
                            act.dma_start(wqk_d[b].rearrange("(k p) n -> p k n", p=P)[:, :, 2 * m * S:2 * (m + 1) * S],
                                          wqk1[:, m % 2, :, b, :]).then_inc(qk1_stored[m % 2], 16)
                        act.wait_ge(vo1_out, 8 * (m + 1))
                        for hh in range(2):
                            h = 2 * m + hh
                            act.dma_start(vwo_d[:, h * S:(h + 1) * S, :].rearrange("b s n -> s b n"),
                                          vwo1[:, m % 2, hh, :, :]).then_inc(vo1_stored[m % 2], 16)

                    load_heads(0)
                    load_heads(1)
                    act.dma_start(wgu0[:], io["wgu0"].rearrange("(k p) n -> p k n", p=P)).then_inc(ffn0_w_in, 16)
                    act.dma_start(wd0[:], io["wd0"].rearrange("(u p) n -> p u n", p=P)).then_inc(ffn0_w_in, 16)
                    act.dma_start(wr0[:], io["wr0"].rearrange("(k p) n -> p k n", p=P)).then_inc(ffn0_w_in, 16)
                    act.wait_ge(w0_in, 96)
                    for m in range(KD):
                        act.wait_ge(fold_mm, m + 1)
                        act.activation(kT0[:, m, :], bank[:, m, 0:BS], ACT.Identity, bias=bias0[:, 1, m:m + 1])\
                           .then_inc(kT0_ready, 1)
                    for m in range(KD):
                        act.wait_ge(fold_mm, KD + m + 1)
                        act.activation(vT0[:, m, :], bank[:, 2 + m, 0:BS], ACT.Identity, bias=bias0[:, 2, m:m + 1])\
                           .then_inc(vT0_ready, 1)
                    act.wait_ge(fold_out, 3)
                    ln_evict_job(act, 0, 0)
                    for c in range(CHUNKS):
                        if c + 1 < CHUNKS:
                            want(act, s_mm, c)
                            ln_evict_job(act, c + 1, (c + 1) % 2)
                        act.wait_ge(s_mm, c + 1)
                        want(act, s_stored[c % 2], 32 * (c // 2))
                        act.activation(sT[:, c % 2, :], bank[0:S, 2 + c % 2, :], ACT.Identity,
                                       bias=bqk[:, c // 2:c // 2 + 1]).then_inc(s_out, 1)
                        act.wait_ge(kv1_mm, 2 * c + 1)
                        want(act, vo1_mm, 8 * (c - 1))
                        act.activation(kT1[:, c % 2, :], bank[:, 4, 0:BS], ACT.Copy, scale=DK ** -0.5).then_inc(k1_out, 1)
                        act.wait_ge(kv1_mm, 2 * c + 2)
                        act.activation(vT1[:, c % 2, :], bank[:, 5, 0:BS], ACT.Copy).then_inc(v1_out, 1)
                        if c >= 1:
                            store_heads(c - 1)
                            if c + 1 < CHUNKS:
                                load_heads(c + 1)
                    store_heads(CHUNKS - 1)
                    act.wait_ge(nm_ready, 1)
                    act.activation(expm, mean[:], ACT.Exp, bias=negmax[:, 0:1]).then_inc(ex_ready, 1)
                    for par in range(2):
                        act.wait_ge(qk1_stored[par], 16 * B * 4)
                        act.wait_ge(vo1_stored[par], 16 * 2 * 4)
                    act.wait_ge(ffn0_w_in, 48)

                @block.vector
                def _(dve):
                    step = Chain(dve, d1, passed)
                    for m in range(KD):
                        dve.wait_ge(fold_mm, 2 * KD + m + 1)
                        dve.tensor_copy(wqk0[:, m, :], bank[:, 4 + m, 0:BS]).then_inc(fold_out, 1)
                    dve.wait_ge(fold_mm, 3 * KD + 1)
                    dve.tensor_copy(bqk[:], bank[0:S, 6, 0:B]).then_inc(fold_out, 1)
                    for b in range(B):
                        dve.wait_ge(vwo_mm, b + 1)
                        dve.tensor_copy(vwo0[0:S, b, :], bank[0:S, 4 + b, 0:D]).then_inc(vwo_out, 1)
                    dve.wait_ge(tg_ready, 1)

                    def fold_heads(m):
                        want(dve, qk1_stored[m % 2], 16 * B * (m // 2))
                        want(dve, vo1_stored[m % 2], 16 * 2 * (m // 2))
                        for hh in range(2):
                            for k in range(KD):
                                n = 2 * hh + k
                                dve.wait_ge(qk1_mm, 4 * m + n + 1)
                                dve.tensor_copy(wqk1[:, m % 2, k, :, hh * S:(hh + 1) * S],
                                                bank[:, 6 + n % 2, 0:BS].rearrange("p (b s) -> p b s", b=B))\
                                   .then_inc(qk1_out, 1)
                        for hh in range(2):
                            for b in range(B):
                                n = 4 * hh + b
                                dve.wait_ge(vo1_mm, 8 * m + n + 1)
                                dve.tensor_scalar(vwo1[:, m % 2, hh, b, :], bank[0:S, 6 + n % 2, 0:D],
                                                  tg[0:S, 1:2], None, ALU.mult).then_inc(vo1_out, 1)

                    for c in range(2):
                        dve.wait_ge(x_in[c], 16)
                        ln_stats_job(dve, c, c, c % 2)
                        ln_norm_job(dve, c, c, c % 2)
                    for c in range(CHUNKS):
                        if c + 2 < CHUNKS:
                            dve.wait_ge(x_in[c + 2], 16)
                            ln_stats_job(dve, c + 2, c + 2, c % 2)
                        if c >= 1:
                            fold_heads(c - 1)
                        if c + 2 < CHUNKS:
                            ln_norm_job(dve, c + 2, c + 2, c % 2)
                    fold_heads(CHUNKS - 1)
                    dve.wait_ge(bo_in, 64)
                    dve.wait_ge(vwo_out, B)
                    dve.tensor_scalar(vwo0[:], vwo0[:], tg[0:S + 1, 0:1], None, ALU.mult).then_inc(vwo_out, 1)
                    dve.wait_ge(uv_mm, B)
                    uv = bank[:, 2, 0:B * 16].rearrange("p (b c u) -> p c b u", b=B, u=2)
                    dve.tensor_copy(sumU[:], uv[:, :, :, 0]).then_inc(uv_out, 1)
                    dve.tensor_copy(difV[:], uv[:, :, :, 1]).then_inc(uv_out, 1)
                    dve.wait_ge(h_mm, 1)
                    step(dve.tensor_copy(urow[:, 0:L], bank[0:B, 0:2, :].rearrange("p a n -> p (a n)")))
                    step(dve.tensor_copy(urow[:, L:L + 1], urow[:, 0:1]))
                    step(dve.tensor_tensor(even[:], urow[:, 0:L], urow[:, L:0:-1], ALU.add))
                    odd = bank[0:B, 3, :]
                    c4 = 1.0 / (4 * D)
                    step(dve.scalar_tensor_tensor(mean[:, 0:CHUNK], even[:, 0:CHUNK], c4, odd, ALU.mult, ALU.add))
                    step(dve.tensor_scalar(mean[:, CHUNK:CHUNK + 1], even[:, CHUNK:CHUNK + 1], c4, None, ALU.mult))
                    step(dve.scalar_tensor_tensor(mean[:, CHUNK + 1:L], even[:, CHUNK + 1:L], c4,
                                                  odd[:, CHUNK - 1:0:-1], ALU.mult, ALU.subtract))
                    step(dve.max(top[:, 0:8], mean[:]))
                    step(dve.match_replace(left1[:], top[:, 0:8], mean[:], NEG))
                    step(dve.max(top[:, 8:16], left1[:]))
                    step(dve.memset(top[:, TOPK:16], SENTINEL))
                    step(dve.match_replace(left2[:], top[:, 8:16], left1[:], NEG))
                    dve.tensor_scalar(negmax[:], top[:, 0:1], -1.0, None, ALU.mult).then_inc(nm_ready, 1)
                    dve.wait_ge(ex_ready, 1)
                    step(dve.scalar_tensor_tensor(wsel[:], left2[:], NEG, expm, ALU.is_equal, ALU.mult,
                                                  accum_out=wsum[:, 0:1]))
                    step(dve.reciprocal(wsum[:, 1:2], wsum[:, 0:1]))
                    dve.tensor_scalar(wrow[:, 0:S], wsel[:, S - 1::-1], wsum[:, 1:2], None, ALU.mult).then_inc(w_ready, 1)
                    dve.tensor_scalar(wrow[:, S:WROW], wsel[:, L - 1:0:-1], wsum[:, 1:2], None, ALU.mult)\
                       .then_inc(w_ready, 1)

                @block.tensor
                def _(pe):
                    pe.wait_ge(w0_in, 96)
                    for base, w in ((0, wk0), (2, wv0)):
                        for m in range(KD):
                            for k in range(KD):
                                last = pe.matmul(bank[:, base + m, 0:BS], w[:, k, m * P:(m + 1) * P], ctxT[:, k, :],
                                                 start=k == 0, stop=k == KD - 1)
                            last.then_inc(fold_mm, 1)
                    pe.wait_ge(kT0_ready, KD)
                    for m in range(KD):
                        for k in range(KD):
                            last = pe.matmul(bank[:, 4 + m, 0:BS], wqT0[:, k, m * P:(m + 1) * P], kT0[:, k, :],
                                             start=k == 0, stop=k == KD - 1)
                        last.then_inc(fold_mm, 1)
                    for b in range(B):
                        for k in range(KD):
                            last = pe.matmul(bank[0:S, 6, b:b + 1], kT0[:, k, b * S:(b + 1) * S], bias0[:, 0, k:k + 1],
                                             start=k == 0, stop=k == KD - 1)
                    last.then_inc(fold_mm, 1)
                    pe.wait_ge(vT0_ready, KD)
                    pe.wait_ge(fold_out, 3)
                    for b in range(B):
                        for k in range(KD):
                            last = pe.matmul(bank[0:S, 4 + b, 0:D], vT0[:, k, b * S:(b + 1) * S], wo0[:, k, :],
                                             start=k == 0, stop=k == KD - 1)
                        last.then_inc(vwo_mm, 1)
                    pe.wait_ge(ident_ready, 1)
                    pe.wait_ge(consts_ready, 3)

                    def scores(c):
                        pe.wait_ge(ln_xT, 2 * c + 2)
                        want(pe, s_out, c - 1)
                        for k in range(KD):
                            last = pe.matmul(bank[0:S, 2 + c % 2, :], wqk0[:, k, (c // 2) * S:(c // 2 + 1) * S],
                                             xnT[:, c % 2, k, :], start=k == 0, stop=k == KD - 1)
                        last.then_inc(s_mm, 1)

                    def keys_values(m):
                        pe.wait_ge(w1_in[m % 2], 64 * (m // 2 + 1))
                        for n, (w, done) in enumerate(((wk1, k1_out), (wv1, v1_out))):
                            want(pe, done, m)
                            for k in range(KD):
                                last = pe.matmul(bank[:, 4 + n, 0:BS], w[:, m % 2, k, :], ctxT[:, k, :],
                                                 start=k == 0, stop=k == KD - 1)
                            last.then_inc(kv1_mm, 1)

                    def fold_heads(m):
                        pe.wait_ge(k1_out, m + 1)
                        for hh in range(2):
                            rows = slice(hh * DK, (hh + 1) * DK)
                            for k in range(KD):
                                n = 2 * hh + k
                                want(pe, qk1_out, 4 * m + n - 1)
                                if n < 2:
                                    want(pe, vo1_out, 8 * m - 1 + n)
                                pe.matmul(bank[:, 6 + n % 2, 0:BS], wqT1[rows, m % 2, k * P:(k + 1) * P],
                                          kT1[rows, m % 2, :], start=True, stop=True).then_inc(qk1_mm, 1)
                        pe.wait_ge(v1_out, m + 1)
                        for hh in range(2):
                            rows = slice(hh * DK, (hh + 1) * DK)
                            for b in range(B):
                                n = 4 * hh + b
                                if n < 2:
                                    pe.wait_ge(qk1_out, 4 * m + 3 + n)
                                else:
                                    pe.wait_ge(vo1_out, 8 * m + n - 1)
                                pe.matmul(bank[0:S, 6 + n % 2, 0:D], vT1[rows, m % 2, b * S:(b + 1) * S],
                                          wo1[rows, m % 2, :], start=True, stop=True).then_inc(vo1_mm, 1)

                    ln_transpose_job(pe, 0, 0)
                    pe.wait_ge(vwo_out, B)
                    for c in range(CHUNKS):
                        if c + 1 < CHUNKS:
                            ln_transpose_job(pe, c + 1, (c + 1) % 2)
                        scores(c)
                        keys_values(c)
                        if c >= 1:
                            fold_heads(c - 1)
                    fold_heads(CHUNKS - 1)
                    pe.wait_ge(s_out, CHUNKS)
                    for b in range(B):
                        pe.wait_ge(skew_in[b % 2], 32 * (b // 2 + 1))
                        for c in range(8):
                            for sign in range(2):
                                last = pe.matmul(bank[:, 2, (b * 8 + c) * 2:(b * 8 + c) * 2 + 2],
                                                 skew[:, b % 2, sign, c * P:(c + 1) * P],
                                                 signs[0:S, 2 * sign:2 * sign + 2], start=sign == 0, stop=sign == 1)
                        last.then_inc(uv_mm, 1)
                    pe.wait_ge(uv_out, 2)
                    pe.wait_ge(htab_in, 16)
                    for c in range(8):
                        pe.matmul(bank[0:B, 3, :], difV[:, c, :], htab[:, c, :], start=c == 0, stop=c == 7)
                    pe.wait_ge(ln_xT, 2 * CHUNKS)
                    for c in range(8):
                        last = pe.transpose(bank[0:B, c // 4, (c % 4) * P:(c % 4 + 1) * P], sumU[:, c, :], ident[:])
                    last.then_inc(h_mm, 1)

        mrow = sb("mask_row", [1, B, HS], BF16)
        onerow = sb("onerow", [1, P], BF16)
        wk = sb("wk", [P, TILES, K1])
        two = ExitStack()
        with two:
            mt = sb("shift_mt", [S + 1, 2, CHUNK], at=two)
            sg = sb("silu_gate", [P, 2, CHUNK], at=two)
            prod0 = sb("prod0", [P, 2, CHUNK], at=two)
            wgu_hi = sb("wgu_hi", [P, KD, UNITS * 2 * P], F32R, at=two)
            wgu_lo = sb("wgu_lo", [P, KD, UNITS * 2 * P], F32R, at=two)
            wd_hi = sb("wd_hi", [P, UNITS, D], F32R, at=two)
            wd_lo = sb("wd_lo", [P, UNITS, D], F32R, at=two)
            wr_hi = sb("wr_hi", [P, KD, R0], F32R, at=two)
            wr_lo = sb("wr_lo", [P, KD, R0], F32R, at=two)
            x_hi = sb("x_hi", [P, 2, KD, CHUNK], F32R, at=two)
            x_lo = sb("x_lo", [P, 2, KD, CHUNK], F32R, at=two)
            act_hi = sb("act_hi", [P, 2, CHUNK], F32R, at=two)
            act_lo = sb("act_lo", [P, 2, CHUNK], F32R, at=two)
            w_hi_ready, w_lo_ready, wd_lo_ready, x_hi_ready = (sem("w_hi_ready"), sem("w_lo_ready"), sem("wd_lo_ready"),
                                                               sem("x_hi_ready"))
            lg = sb("logits", [P, 2, CT, R0], at=two)
            v8 = sb("top8", [P, 2, CT, 8], at=two)
            taken = sb("taken", [P, 2, CT, E0], at=two)
            z = sb("z", [P, 2, 2, CT], at=two)
            th = sb("th", [P, 2, 2, CT], at=two)
            wlow = sb("wlow", [P, 2, CT], at=two)
            pick = sb("pick", [P, 2, CT, E0], at=two)
            cw = sb("cw", [P, 2, CT, E0 + 1], at=two)
            zrow = sb("zrow", [P, ROW], at=two)
            mask_u = sb("mask_u", [1, B * S], io["mask"].dtype, at=two)
            mask_in, mask_done, z_zero, z_done, cleared = (sem("mask_in"), sem("mask_done"), sem("z_zero"), sem("z_done"),
                                                           sem("cleared"))
            mt_ones, mt_in = sem("mt_ones"), [sem("mt_in0"), sem("mt_in1")]
            ap_mm, ap_out, lg_mm, lg_out = sem("ap_mm"), sem("ap_out"), sem("lg_mm"), sem("lg_out")
            z_ready, th_ready, cw_ready = sem("z_ready"), sem("th_ready"), sem("cw_ready")
            CR = 2
            gate_mm, up_mm, sg_ready, prod_ready, hi_ready, lo_ready, down_mm, unit_added = (
                sem("gate_mm"), sem("up_mm"), sem("sg_ready"), sem("prod_ready"), sem("hi_ready"), sem("lo_ready"),
                sem("down_mm"), sem("unit_added"))
            d2 = sem("dve_steps_2")
            QB = CHUNKS

            def chunks_pipelined(eng, prepare, main, chain=None, per=0):
                prepare(0, 0)
                with eng.Fori(0, CHUNKS // 2 - 1) as i:
                    if chain:
                        chain.enter(i, per)
                    main(2 * i, 0, 2 * i + 1)
                    main(2 * i + 1, 1, 2 * i + 2)
                if chain:
                    chain.leave(CHUNKS // 2 - 1)
                main(CHUNKS - 2, 0, CHUNKS - 1)
                main(CHUNKS - 1, 1, None)

            with nc.Block() as block:
                @block.sync
                def _(sp):
                    sp.wait_ge(z_done, 1)
                    over = slots_d.rearrange("(p r) w -> p r w", p=P)
                    R = SLOTS // P
                    sp.dma_start(over, bass.AP(zrow[:].tensor, 0, [[ROW, P], [0, R], [1, ROW]])).then_inc(cleared, 16)
                    over = y_d.rearrange("(p r) w -> p r w", p=P)
                    R = T * K1 // P
                    for half in range(2):
                        sp.dma_start(over[:, half * R // 2:(half + 1) * R // 2, :],
                                     bass.AP(zrow[:].tensor, 0, [[ROW, P], [0, R // 2], [1, D]])).then_inc(cleared, 16)
                    sp.dma_start(mask_u[:], io["mask"].rearrange("b s -> (b s)").rearrange("(a n) -> a n", a=1))\
                      .then_inc(mask_in, 16)
                    sp.wait_ge(mt_ones, 1)
                    for c in range(2):
                        sp.dma_start(mt[0:S, c, :], bass.AP(w_d.tensor, c * CHUNK, [[1, S], [1, CHUNK]])).then_inc(mt_in[c], 16)
                    with sp.Fori(0, CHUNKS // 2 - 1) as i:
                        for par in range(2):
                            sp.wait_ge(ap_mm, 2 * i + (par + 1))
                            rows = bass.AP(w_d.tensor, par * CHUNK, [[WROW, B], [1, S], [1, CHUNK]])
                            sp.dma_start(mt[0:S, par, :], rows[bass.ds(i + 1, 1), :, :]).then_inc(mt_in[par], 16)
                    for par in range(2):
                        sp.wait_ge(mt_in[par], 16 * (CHUNKS // 2))
                    sp.wait_ge(cleared, 48)

                @block.gpsimd
                def _(pool):
                    pool.sem_inc(lo_ready, CR)
                    pool.memset(zrow[:], 0.0).then_inc(z_zero, 1)
                    pool.memset(onerow[:], 1.0).then_inc(mask_done, 1)
                    pool.wait_ge(z_zero, 1)
                    pool.memset(zrow[:, D:D + 1].bitcast(I32), int(FAR)).then_inc(z_done, 1)
                    pool.wait_ge(w_hi_ready, 2 * UNITS + 1)
                    pool.tensor_tensor(wd_lo[:], wd0[:], wd_hi[:].bitcast(F32), ALU.subtract).then_inc(wd_lo_ready, 1)
                    pool.wait_ge(mask_in, 16)
                    for b in range(B):
                        pool.tensor_scalar(mrow[:, b, :].rearrange("p (h s) -> p h s", h=H1),
                                           mask_u[:, b * S:(b + 1) * S].rearrange("p (a s) -> p a s", a=1)
                                           .broadcast_to([1, H1, S]), MASKED, None, ALU.mult).then_inc(mask_done, 1)

                    def low_part(c, u):
                        g = UNITS * c + u
                        pool.wait_ge(hi_ready, g + (CR + 1))
                        pool.wait_ge(down_mm, g + (CR - 1))
                        pool.tensor_tensor(act_lo[:, u % 2, :], prod0[:, u % 2, :], act_hi[:, u % 2, :].bitcast(F32),
                                           ALU.subtract).then_inc(lo_ready, 1)

                    def prepare(c, par):
                        ln_rstd_job(pool, c + QB, par)
                        low_part(c, 0)
                        low_part(c, 1)

                    def main(c, par, nxt):
                        for u in range(2, UNITS):
                            low_part(c, u)
                            if nxt is not None and u == 3:
                                ln_rstd_job(pool, nxt + QB, 1 - par)
                        if nxt is not None:
                            low_part(nxt, 0)
                            low_part(nxt, 1)

                    chunks_pipelined(pool, prepare, main)

                @block.scalar
                def _(act):
                    act.sem_inc(sg_ready, CR)
                    act.sem_inc(hi_ready, CR)
                    act.activation(wr_hi[:], wr0[:], ACT.Copy).then_inc(w_hi_ready, 1)
                    for u in range(UNITS):
                        cols = slice(2 * u * P, 2 * (u + 1) * P)
                        act.activation(wgu_hi[:, :, cols], wgu0[:, :, cols], ACT.Copy).then_inc(w_hi_ready, 1)
                    for u in range(UNITS):
                        act.activation(wd_hi[:, u, :], wd0[:, u, :], ACT.Copy).then_inc(w_hi_ready, 1)

                    def evict(c, par):
                        act.wait_ge(ln_T, c + (QB + 1))
                        want(act, up_mm, UNITS * c - (UNITS - CR))
                        for k in range(KD):
                            act.activation(x_hi[:, par, k, :], bank[:, k, :], ACT.Copy).then_inc(x_hi_ready, 1)

                    def tanh(c, par):
                        act.wait_ge(z_ready, c + 1)
                        want(act, cw_ready, c - 1)
                        act.activation(th[:, par, :, :], z[:, par, :, :], ACT.Tanh, scale=0.5).then_inc(th_ready, 1)

                    def unit(c, u):
                        g = UNITS * c + u
                        act.wait_ge(gate_mm, g + (CR + 1))
                        act.wait_ge(prod_ready, g + (CR - 1))
                        act.activation(sg[:, u % 2, :], bank[:, 4 + u % 2, :], ACT.Silu).then_inc(sg_ready, 1)
                        act.wait_ge(prod_ready, g + (CR + 1))
                        act.wait_ge(down_mm, g + (CR - 1))
                        act.activation(act_hi[:, u % 2, :], prod0[:, u % 2, :], ACT.Copy).then_inc(hi_ready, 1)

                    def prepare(c, par):
                        evict(c, par)
                        tanh(c, par)
                        unit(c, 0)
                        unit(c, 1)

                    def main(c, par, nxt):
                        for u in range(2, UNITS):
                            unit(c, u)
                            if nxt is not None and u == 5:
                                evict(nxt, 1 - par)
                            if nxt is not None and u == 10:
                                tanh(nxt, 1 - par)
                        if nxt is not None:
                            unit(nxt, 0)
                            unit(nxt, 1)

                    chunks_pipelined(act, prepare, main)

                @block.vector
                def _(dve):
                    step = Chain(dve, d2, passed)
                    dve.sem_inc(prod_ready, CR)
                    dve.sem_inc(unit_added, CR)
                    dve.memset(mt[64:S + 1, :, :], 1.0).then_inc(mt_ones, 1)
                    dve.wait_ge(w_hi_ready, 1)
                    dve.tensor_tensor(wr_lo[:], wr0[:], wr_hi[:].bitcast(F32), ALU.subtract).then_inc(w_lo_ready, 1)
                    for u in range(UNITS):
                        dve.wait_ge(w_hi_ready, u + 2)
                        cols = slice(2 * u * P, 2 * (u + 1) * P)
                        dve.tensor_tensor(wgu_lo[:, :, cols], wgu0[:, :, cols], wgu_hi[:, :, cols].bitcast(F32),
                                          ALU.subtract).then_inc(w_lo_ready, 1)

                    def add_attention(c, par):
                        dve.wait_ge(ap_mm, c + 1)
                        dve.tensor_tensor(x[:, bass.ds(c * CT, CT), :], x[:, bass.ds(c * CT, CT), :],
                                          bank[:, 0:2, :].rearrange("p a (t n) -> p (a t) n", n=D), ALU.add).then_inc(ap_out, 1)
                        dve.wait_ge(ap_out, c + 1)
                        ln_stats_job(dve, c + QB, c, par)

                    def route(c, par):
                        dve.wait_ge(lg_mm, c + 1)
                        dve.tensor_copy(lg[:, par, :, :], bank[:, 0, 0:CT * R0].rearrange("p (t e) -> p t e", e=R0))\
                           .then_inc(lg_out, 1)
                        wait_apart(dve, lg_out, c + 1, passed)
                        for t in range(CT):
                            last = dve.max(v8[:, par, t, :], lg[:, par, t, 0:E0])
                        step(last)
                        dve.tensor_tensor(z[:, par, 0, :], v8[:, par, :, 0], v8[:, par, :, 1], ALU.subtract)
                        dve.tensor_copy(z[:, par, 1, :], lg[:, par, :, E0]).then_inc(z_ready, 1)
                        step(dve.memset(v8[:, par, :, 2:8], SENTINEL))
                        for t in range(CT):
                            last = dve.match_replace(taken[:, par, t, :], v8[:, par, t, :], lg[:, par, t, 0:E0], NEG)
                        step(last)

                    def weigh(c, par):
                        def over(ap):
                            return ap.rearrange("p (t a) -> p t a", a=1).broadcast_to([P, CT, E0])
                        dve.wait_ge(th_ready, c + 1)
                        step(dve.tensor_scalar(wlow[:, par, :], th[:, par, 0, :], -0.5, 0.5, ALU.mult, ALU.add))
                        step(dve.tensor_tensor(pick[:, par, :, :], lg[:, par, :, 0:E0], over(v8[:, par, :, 0]), ALU.is_equal))
                        step(dve.tensor_tensor(pick[:, par, :, :], pick[:, par, :, :], over(th[:, par, 0, :]), ALU.mult))
                        step(dve.tensor_tensor(pick[:, par, :, :], pick[:, par, :, :], over(wlow[:, par, :]), ALU.add))
                        dve.scalar_tensor_tensor(cw[:, par, :, 0:E0], taken[:, par, :, :], NEG, pick[:, par, :, :],
                                                 ALU.is_equal, ALU.mult)
                        step(dve.tensor_scalar(cw[:, par, :, E0], th[:, par, 1, :], 0.5, 0.5, ALU.mult, ALU.add))
                        dve.tensor_scalar(cw[:, par, :, :], cw[:, par, :, :], tg[:, 2:3], None, ALU.mult).then_inc(cw_ready, 1)

                    def low_parts(c, par):
                        dve.wait_ge(x_hi_ready, 2 * c + 2)
                        want(dve, up_mm, UNITS * c - (UNITS - CR))
                        for k in range(KD):
                            dve.tensor_tensor(x_lo[:, par, k, :], bank[:, k, :], x_hi[:, par, k, :].bitcast(F32),
                                              ALU.subtract).then_inc(ln_xT, 1)

                    def product(c, u):
                        g = UNITS * c + u
                        dve.wait_ge(up_mm, g + (CR + 1))
                        dve.wait_ge(sg_ready, g + (CR + 1))
                        dve.wait_ge(lo_ready, g + (CR - 1))
                        dve.tensor_tensor(prod0[:, u % 2, :], bank[:, 6 + u % 2, :], sg[:, u % 2, :], ALU.mult)\
                           .then_inc(prod_ready, 1)

                    def add_unit(c, par, u):
                        g = UNITS * c + u
                        if u == 0:
                            dve.wait_ge(cw_ready, c + 1)
                        dve.wait_ge(down_mm, g + (CR + 1))
                        dve.wait_ge(unit_added, g + CR)
                        for t in range(CT):
                            row = x[:, bass.ds(c * CT + t, 1), :].rearrange("p a n -> p (a n)")
                            last = dve.scalar_tensor_tensor(row, bank[:, 2 + t // 2, (t % 2) * D:(t % 2 + 1) * D],
                                                            cw[:, par, t, min(u, E0):min(u, E0) + 1], row,
                                                            ALU.mult, ALU.add)
                        last.then_inc(unit_added, 1)

                    def prepare(c, par):
                        add_attention(c, par)
                        ln_norm_job(dve, c + QB, c, par)
                        low_parts(c, par)
                        route(c, par)
                        weigh(c, par)
                        product(c, 0)
                        product(c, 1)

                    def main(c, par, nxt):
                        for u in range(2, UNITS + 2):
                            if u < UNITS:
                                product(c, u)
                            elif nxt is not None:
                                product(nxt, u - UNITS)
                            add_unit(c, par, u - 2)
                            if nxt is not None:
                                if u == 2:
                                    add_attention(nxt, 1 - par)
                                if u == 4:
                                    ln_norm_job(dve, nxt + QB, nxt, 1 - par)
                                if u == 6:
                                    low_parts(nxt, 1 - par)
                                if u == 9:
                                    route(nxt, 1 - par)
                                if u == 11:
                                    weigh(nxt, 1 - par)

                    chunks_pipelined(dve, prepare, main, step, 16)

                @block.tensor
                def _(pe):
                    pe.sem_inc(gate_mm, CR)
                    pe.sem_inc(up_mm, CR)
                    pe.sem_inc(down_mm, CR)

                    def product3(to, a_hi, a_lo, b_hi, b_lo, start, stop):
                        pe.matmul(to, a_hi, b_hi, start=start, stop=False)
                        pe.matmul(to, a_hi, b_lo, start=False, stop=False)
                        return pe.matmul(to, a_lo, b_hi, start=False, stop=stop)

                    def attention(c, par):
                        pe.wait_ge(mt_in[par], 16 * (c // 2) + 16)
                        want(pe, lg_out, c)
                        for t in range(CT):
                            last = pe.matmul(bank[:, t // 2, (t % 2) * D:(t % 2 + 1) * D], mt[:, par, t * P:(t + 1) * P],
                                             vwo0[:, bass.ds(c // 2, 1), :].rearrange("p a n -> p (a n)"),
                                             start=True, stop=True)
                        last.then_inc(ap_mm, 1)

                    def logits(c, par):
                        pe.wait_ge(ln_xT, 2 * c + (2 * QB + 2))
                        for t in range(CT):
                            for k in range(KD):
                                tok = slice(t * P, (t + 1) * P)
                                last = product3(bank[:, 0, t * R0:(t + 1) * R0], x_hi[:, par, k, tok], x_lo[:, par, k, tok],
                                                wr_hi[:, k, :], wr_lo[:, k, :], k == 0, k == KD - 1)
                        last.then_inc(lg_mm, 1)

                    def gate_up(c, par, u):
                        g = UNITS * c + u
                        for half, free, done, to in ((0, sg_ready, gate_mm, 4), (1, prod_ready, up_mm, 6)):
                            pe.wait_ge(free, g + (CR - 1))
                            cols = slice((2 * u + half) * P, (2 * u + half + 1) * P)
                            for k in range(KD):
                                last = product3(bank[:, to + u % 2, :], wgu_hi[:, k, cols], wgu_lo[:, k, cols],
                                                x_hi[:, par, k, :], x_lo[:, par, k, :], k == 0, k == KD - 1)
                            last.then_inc(done, 1)

                    def down(c, u):
                        g = UNITS * c + u
                        pe.wait_ge(lo_ready, g + (CR + 1))
                        pe.wait_ge(unit_added, g + CR)
                        for t in range(CT):
                            tok = slice(t * P, (t + 1) * P)
                            last = product3(bank[:, 2 + t // 2, (t % 2) * D:(t % 2 + 1) * D], act_hi[:, u % 2, tok],
                                            act_lo[:, u % 2, tok], wd_hi[:, u, :], wd_lo[:, u, :], True, True)
                        last.then_inc(down_mm, 1)

                    def prepare(c, par):
                        attention(c, par)
                        ln_transpose_job(pe, c + QB, par)
                        pe.wait_ge(w_lo_ready, UNITS + 1)
                        logits(c, par)
                        gate_up(c, par, 0)
                        gate_up(c, par, 1)
                        pe.wait_ge(wd_lo_ready, 1)

                    def main(c, par, nxt):
                        for u in range(2, UNITS + 2):
                            if u < UNITS:
                                gate_up(c, par, u)
                            elif nxt is not None:
                                gate_up(nxt, 1 - par, u - UNITS)
                            down(c, u - 2)
                            if nxt is not None:
                                if u == 2:
                                    attention(nxt, 1 - par)
                                if u == 5:
                                    ln_transpose_job(pe, nxt + QB, 1 - par)
                                if u == 8:
                                    logits(nxt, 1 - par)

                    chunks_pipelined(pe, prepare, main)

        three = ExitStack()
        with three:
            JC = -(-HS // P)
            JL = HS - (JC - 1) * P
            SPLIT = [(0, 6), (6, 5), (11, 5)]
            wqk = sb("wqk", [P, 2, KD, HS], at=three)
            vwo = sb("vwo", [P, 2, JC, D], at=three)
            sgu = sb("shared_gate_up", [P, KD, 2 * P], at=three)
            sdn = sb("shared_down", [P, D], at=three)
            wr1 = sb("wr1", [P, KD, E1], at=three)
            tri = sb("tri", [P, P], BF16, at=three)
            allone = sb("allone", [P, P], BF16, at=three)
            ebase = sb("ebase", [P, E1], at=three)
            kth = sb("kth", [P, K1, E1], at=three)
            onesf = sb("onesf", [P, E1], at=three)
            outrow = sb("outrow", [P, TILES, K1], I32, at=three)
            ln = {}
            for s in "ab":
                ln[s] = dict(bst=sb(f"bst_{s}", [P, 2, 6], at=three), mv=sb(f"mv_{s}", [P, 2, 2], at=three),
                             veps=sb(f"veps_{s}", [P, 2, 1], at=three), rstd=sb(f"rstd_{s}", [P, 2, 1], at=three),
                             summed=sem(f"{s}_summed"), stats=sem(f"{s}_stats"), eps=sem(f"{s}_eps"),
                             ready=sem(f"{s}_rstd_ready"))
            xa = sb("xa", [P, 2, D], at=three)
            xaT = sb("xaT", [P, 2, KD, P], at=three)
            rows = sb("rows", [P, 2, K1, ROW], at=three)
            xbT = sb("xbT", [P, 2, KD, P], at=three)
            att = sb("att", [P, 2, HS], at=three)
            attT = sb("attT", [P, 2, JC, P], at=three)
            mx = sb("mx", [P, 2, 2, H1], at=three)
            den = sb("den", [P, 2, 2, H1], at=three)
            lg1 = sb("lg1", [P, 2, E1], at=three)
            t8 = sb("t8", [P, 2, 8], at=three)
            ngm = sb("ngm", [P, 2, 1], at=three)
            tk = sb("tk", [P, 2, E1], at=three)
            ew = sb("ew", [P, 2, E1], at=three)
            msel = sb("msel", [P, 2, E1], at=three)
            mselb = sb("mselb", [P, 2, E1], BF16, at=three)
            cum = sb("cum", [P, 2, E1], BF16, at=three)
            ws1 = sb("ws1", [P, 2, 2], at=three)
            wn = sb("wn", [P, 2, E1], at=three)
            key = sb("key", [P, 2, E1], at=three)
            hot = sb("hot", [P, 2, K1, E1], at=three)
            prod = sb("prod", [P, 2, K1, E1], at=three)
            far = sb("far", [P, 2, E1], at=three)
            slot = sb("slot", [P, 2, E1], at=three)
            slotk = sb("slotk", [P, 2, K1], at=three)
            place = sb("place", [P, 2, K1], I32, at=three)
            thg = sb("thg", [P, 2, P], at=three)
            hid = sb("hid", [P, 2, P], at=three)
            actS = sb("actS", [P, 2, P], at=three)

            w3_in, wqk_in, vwo_in = sem("w3_in"), sem("wqk_in"), sem("vwo_in")
            c3, c3_zero = sem("consts3"), sem("consts3_zero")
            a_xn, a_T, a_xT = sem("a_xn"), sem("a_T"), sem("a_xT")
            e_mm, mx_ready, exp_done, den_ready, att_ready = (sem("e_mm"), sem("mx_ready"), sem("exp_done"),
                                                              sem("den_ready"), sem("att_ready"))
            at_T, at_out, av_mm, av_added = sem("at_T"), sem("at_out"), sem("av_mm"), sem("av_added")
            b_xn, b_T, b_xT = sem("b_xn"), sem("b_T"), sem("b_xT")
            r_mm, r_out, ngm_ready, ew_ready, msel_ready = (sem("r_mm"), sem("r_out"), sem("ngm_ready"),
                                                            sem("ew_ready"), sem("msel_ready"))
            thg_ready, actS_ready, sd_mm, sd_added = (sem("thg_ready"), sem("actS_ready"),
                                                             sem("sd_mm"), sem("sd_added"))
            pos_mm, pos_read, place_ready = sem("pos_mm"), sem("pos_read"), sem("place_ready")
            sent = [sem("sent0"), sem("sent1")]
            d3 = sem("dve_steps_3")

            def steps_pipelined(eng, first, step_fn, chain=None, per=0):
                first()
                def run(n, par):
                    step_fn(n, par, n < TILES, 1 <= n <= TILES, 2 <= n < TILES + 2, 3 <= n)
                for n in range(4):
                    run(n, n % 2)
                rounds = (TILES - 6) // 2
                with eng.Fori(0, rounds) as i:
                    if chain:
                        chain.enter(i, per)
                    for par in range(2):
                        step_fn(2 * i + (4 + par), par, True, True, True, True)
                if chain:
                    chain.leave(rounds)
                for n in range(TILES - 2, TILES + 3):
                    run(n, n % 2)

            def tile(n):
                return x[:, bass.ds(n, 1), :].rearrange("p a n -> p (a n)")

            def ln_stats_tile(dve, s, n, par):
                r = ln[s]
                dve.bn_stats(r["bst"][:, par, :], tile(n)).then_inc(r["summed"], 1)
                wait_apart(dve, r["summed"], n + 1, passed)
                dve.bn_aggr(r["mv"][:, par, :], r["bst"][:, par, :]).then_inc(r["stats"], 1)

            def ln_rstd_tile(pool, s, n, par):
                r = ln[s]
                wait_apart(pool, r["stats"], n + 1, passed_pool)
                pool.tensor_scalar_add(r["veps"][:, par, :], r["mv"][:, par, 1:2], EPS).then_inc(r["eps"], 1)
                pool.wait_ge(r["eps"], n + 1)
                pool.tensor_tensor(r["rstd"][:, par, :], r["veps"][:, par, :], neghalf[:, 0:1], ALU.pow)\
                    .then_inc(r["ready"], 1)

            with nc.Block() as block:
                @block.sync
                def _(sp):
                    sp.dma_start(sgu[:], io["sgu1"].rearrange("(k p) n -> p k n", p=P)).then_inc(w3_in, 16)
                    sp.dma_start(sdn[:], io["sd1"]).then_inc(w3_in, 16)
                    sp.dma_start(wr1[:], io["wr1"].rearrange("(k p) n -> p k n", p=P)).then_inc(w3_in, 16)
                    for b in range(B):
                        if b >= 2:
                            sp.wait_ge(e_mm, 8 * (b - 1))
                        sp.dma_start(wqk[:, b % 2, :, :], wqk_d[b].rearrange("(k p) n -> p k n", p=P)).then_inc(wqk_in, 16)
                        sp.wait_ge(wqk_in, 16 * (b + 1))
                        if b >= 2:
                            sp.wait_ge(av_mm, 8 * (b - 1))
                        sp.dma_start(vwo[:, b % 2, 0:JC - 1, :],
                                     vwo_d[b, 0:(JC - 1) * P, :].rearrange("(j p) n -> p j n", p=P)).then_inc(vwo_in, 16)
                        sp.dma_start(vwo[0:JL, b % 2, JC - 1, :], vwo_d[b, (JC - 1) * P:HS, :]).then_inc(vwo_in, 16)
                        sp.wait_ge(vwo_in, 32 * (b + 1))
                    sp.wait_ge(w3_in, 48)

                @block.gpsimd
                def _(pool):
                    def first():
                        pool.memset(tri[:], 1.0).then_inc(c3_zero, 1)
                        pool.memset(allone[:], 1.0).then_inc(c3, 1)
                        pool.memset(onesf[:], 1.0).then_inc(c3, 1)
                        pool.memset(cum[:, 0, :], 0.0).then_inc(c3, 1)
                        pool.memset(rows[:], 0.0).then_inc(c3, 1)
                        for k in range(K1):
                            pool.memset(kth[:, k, :], 1.0 + k).then_inc(c3, 1)
                        pool.iota(outrow[:], pattern=[[K1 * P, TILES], [1, K1]], base=0, channel_multiplier=K1).then_inc(c3, 1)
                        pool.iota(ebase[:], pattern=[[CAP, E1]], base=0, channel_multiplier=0,
                                  allow_small_or_imprecise_dtypes=True).then_inc(c3, 1)
                        pool.wait_ge(c3_zero, 1)
                        pool.affine_select(out=tri[:], in_=tri[:], compare_op=ALU.is_gt, fill=0.0, base=0,
                                           pattern=[[1, P]], channel_multiplier=-1).then_inc(c3, 1)
                        for n in range(2):
                            ln_rstd_tile(pool, "a", n, n)

                    def step(n, par, scores, values, route, dispatch):
                        if route:
                            ln_rstd_tile(pool, "b", n - 2, par)
                        if dispatch:
                            wait_apart(pool, place_ready, n - 2, passed_pool)
                            for k in range(K1):
                                pool.indirect_dma_start(
                                    slots_d, bass.IndirectOffsetOnAxis(ap=place[:, 1 - par, k:k + 1], axis=0),
                                    rows[:, 1 - par, k, :], None, bounds_check=SLOTS - 1, oob_is_err=False)\
                                    .then_inc(sent[1 - par], 16)
                        if scores:
                            pool.wait_ge(den_ready, n + 1)
                            pool.tensor_tensor(att[:, par, :].rearrange("p (h s) -> p h s", h=H1),
                                               att[:, par, :].rearrange("p (h s) -> p h s", h=H1),
                                               den[:, par, 1, :].rearrange("p (h a) -> p h a", a=1)
                                               .broadcast_to([P, H1, S]), ALU.mult).then_inc(att_ready, 1)
                            if not isinstance(n, int) or n + 2 < TILES:
                                ln_rstd_tile(pool, "a", n + 2, par)

                    steps_pipelined(pool, first, step)
                    for par in range(2):
                        pool.wait_ge(sent[par], 16 * K1 * TILES // 2)

                @block.scalar
                def _(act):
                    def evict_a(n, par):
                        act.wait_ge(a_T, n + 1)
                        want(act, e_mm, n - 1)
                        act.activation(xaT[:, par, :, :].rearrange("p k t -> p (k t)"), bank[:, 6, D:2 * D], ACT.Copy)\
                           .then_inc(a_xT, 1)

                    def exps(n, par, a):
                        h0, count = SPLIT[a]
                        if a == 0:
                            act.wait_ge(mx_ready, n + 1)
                            want(act, att_ready, n - 1)
                        for i in range(count):
                            h = h0 + i
                            last = act.activation(att[:, par, h * S:(h + 1) * S], bank[:, a, i * S:(i + 1) * S], ACT.Exp,
                                                  bias=mx[:, par, 1, h:h + 1], accum_out=den[:, par, 0, h:h + 1])
                        last.then_inc(exp_done, 1)

                    def step(n, par, scores, values, route, dispatch):
                        if route:
                            act.wait_ge(b_T, n - 1)
                            want(act, r_mm, n - 3)
                            act.activation(xbT[:, par, :, :].rearrange("p k t -> p (k t)"), bank[:, 6, 0:D], ACT.Copy)\
                               .then_inc(b_xT, 1)
                        if values:
                            for g in range(2):
                                act.wait_ge(at_T, 3 * n + (g - 2))
                                want(act, av_mm, n - 2)
                                act.activation(attT[:, 1 - par, 4 * g:4 * g + 4, :].rearrange("p j t -> p (j t)"),
                                               bank[:, 3 + g, :], ACT.Copy).then_inc(at_out, 1)
                            act.wait_ge(at_T, 3 * n)
                            act.activation(attT[:, 1 - par, 8, :], bank[:, 3, 0:P], ACT.Copy)
                            act.activation(attT[0:JL, 1 - par, 9, :], bank[0:JL, 3, P:2 * P], ACT.Copy).then_inc(at_out, 1)
                        if scores:
                            if not isinstance(n, int) or n + 1 < TILES:
                                evict_a(n + 1, 1 - par)
                            exps(n, par, 0)
                        if route:
                            act.wait_ge(r_out, n - 1)
                            want(act, actS_ready, n - 3)
                            act.activation(thg[:, par, :], bank[:, 7, 0:P], ACT.Tanh, scale=0.5).then_inc(thg_ready, 1)
                            act.wait_ge(ngm_ready, n - 1)
                            act.activation(ew[:, par, :], lg1[:, par, :], ACT.Exp, bias=ngm[:, par, :]).then_inc(ew_ready, 1)
                        if scores:
                            exps(n, par, 1)
                            exps(n, par, 2)

                    steps_pipelined(act, lambda: evict_a(0, 0), step)

                @block.vector
                def _(dve):
                    chain = Chain(dve, d3, passed)

                    def norm_a(n, par):
                        dve.wait_ge(ln["a"]["ready"], n + 1)
                        want(dve, a_T, n - 1)
                        dve.tensor_scalar(xa[:, par, :], tile(n), ln["a"]["mv"][:, par, 0:1], ln["a"]["rstd"][:, par, :],
                                          ALU.subtract, ALU.mult).then_inc(a_xn, 1)

                    def stats_a(n, par):
                        if n is not None:
                            wait_apart(dve, a_xn, n - 1, passed)
                            ln_stats_tile(dve, "a", n, par)

                    def largest(n, par):
                        dve.wait_ge(e_mm, n + 1)
                        want(dve, exp_done, 3 * n - 3)
                        for a, (h, count) in enumerate(SPLIT):
                            e = bank[:, a, 0:count * S].rearrange("p (h s) -> p h s", s=S)
                            last = dve.tensor_reduce(mx[:, par, 0, h:h + count], e, AX.X, ALU.max)
                        chain(last)
                        dve.tensor_scalar(mx[:, par, 1, :], mx[:, par, 0, :], -1.0, None, ALU.mult).then_inc(mx_ready, 1)

                    def denominators(n, par):
                        dve.wait_ge(exp_done, 3 * n + 3)
                        dve.reciprocal(den[:, par, 1, :], den[:, par, 0, :]).then_inc(den_ready, 1)

                    def over_k(ap):
                        return ap.rearrange("p (a e) -> p a e", a=1).broadcast_to([P, K1, E1])

                    def places(n, par):
                        dve.wait_ge(pos_mm, n + 1)
                        pos = bank[:, 7, 288:288 + E1]
                        dve.tensor_scalar(far[:, par, :], pos, float(CAP), FAR, ALU.is_ge, ALU.mult)
                        chain(dve.tensor_tensor(slot[:, par, :], pos, ebase[:], ALU.add))
                        dve.tensor_tensor(slot[:, par, :], slot[:, par, :], far[:, par, :], ALU.add).then_inc(pos_read, 1)
                        dve.wait_ge(pos_read, n + 1)
                        chain(dve.tensor_tensor(prod[:, par, :, :], hot[:, par, :, :], over_k(slot[:, par, :]), ALU.mult))
                        chain(dve.tensor_reduce(slotk[:, par, :], prod[:, par, :, :], AX.X, ALU.add))
                        want(dve, sent[par], 64 * (n // 2))
                        dve.tensor_copy(place[:, par, :], slotk[:, par, :]).then_inc(place_ready, 1)
                        dve.wait_ge(sd_mm, n + 1)
                        dve.scalar_tensor_tensor(tile(n), bank[:, 5, D:2 * D], tg[:, 3:4], tile(n), ALU.mult, ALU.add)\
                           .then_inc(sd_added, 1)

                    def norm_b(n, par):
                        dve.wait_ge(ln["b"]["ready"], n + 1)
                        want(dve, b_T, n - 1)
                        want(dve, sent[par], 64 * (n // 2))
                        src = tile(n).rearrange("p (a n) -> p a n", a=1).broadcast_to([P, K1, D])
                        dve.tensor_copy(rows[:, par, :, D:D + 1].bitcast(I32),
                                        outrow[:, bass.ds(n, 1), :].rearrange("p a k -> p k a"))
                        dve.tensor_scalar(rows[:, par, :, 0:D], src, ln["b"]["mv"][:, par, 0:1], ln["b"]["rstd"][:, par, :],
                                          ALU.subtract, ALU.mult).then_inc(b_xn, 1)

                    def add_values(n, par):
                        dve.wait_ge(av_mm, n + 1)
                        dve.tensor_tensor(tile(n), tile(n), bank[:, 5, 0:D], ALU.add).then_inc(av_added, 1)
                        wait_apart(dve, av_added, n + 1, passed)
                        wait_apart(dve, b_xn, n - 1, passed)
                        ln_stats_tile(dve, "b", n, par)

                    def route(n, par):
                        dve.wait_ge(r_mm, n + 1)
                        dve.tensor_copy(lg1[:, par, :], bank[:, 7, 256:256 + E1]).then_inc(r_out, 1)
                        wait_apart(dve, r_out, n + 1, passed)
                        chain(dve.max(t8[:, par, :], lg1[:, par, :]))
                        dve.tensor_scalar(ngm[:, par, :], t8[:, par, 0:1], -1.0, None, ALU.mult).then_inc(ngm_ready, 1)
                        chain(dve.memset(t8[:, par, K1:8], SENTINEL))
                        chain(dve.match_replace(tk[:, par, :], t8[:, par, :], lg1[:, par, :], NEG))
                        dve.tensor_scalar(mselb[:, par, :], tk[:, par, :], NEG, None, ALU.is_equal)
                        chain(dve.tensor_scalar(msel[:, par, :], tk[:, par, :], NEG, None, ALU.is_equal))
                        dve.tensor_tensor(cum[:, 1 - par, :], cum[:, par, :], mselb[:, par, :], ALU.add).then_inc(msel_ready, 1)
                        chain(dve.tensor_tensor_scan(key[:, par, :], onesf[:], msel[:, par, :], 0.0, ALU.mult, ALU.add))
                        chain(dve.tensor_tensor(key[:, par, :], key[:, par, :], msel[:, par, :], ALU.mult))
                        chain(dve.tensor_tensor(hot[:, par, :, :], over_k(key[:, par, :]), kth[:], ALU.is_equal))
                        dve.wait_ge(ew_ready, n + 1)
                        chain(dve.scalar_tensor_tensor(wn[:, par, :], msel[:, par, :], 1.0, ew[:, par, :],
                                                       ALU.mult, ALU.mult, accum_out=ws1[:, par, 0:1]))
                        chain(dve.reciprocal(ws1[:, par, 1:2], ws1[:, par, 0:1]))
                        chain(dve.tensor_scalar(wn[:, par, :], wn[:, par, :], ws1[:, par, 1:2], tg[:, 3:4], ALU.mult, ALU.mult))
                        chain(dve.tensor_tensor(prod[:, par, :, :], hot[:, par, :, :], over_k(wn[:, par, :]), ALU.mult))
                        chain(dve.tensor_reduce(wk[:, bass.ds(n, 1), :].rearrange("p a k -> p (a k)"),
                                                prod[:, par, :, :], AX.X, ALU.add))
                        dve.wait_ge(thg_ready, n + 1)
                        want(dve, sd_mm, n - 1)
                        chain(dve.scalar_tensor_tensor(hid[:, par, :], thg[:, par, :], 1.0, bank[:, 7, 0:P], ALU.add, ALU.mult))
                        dve.scalar_tensor_tensor(actS[:, par, :], hid[:, par, :], 0.5, bank[:, 7, P:2 * P], ALU.mult, ALU.mult)\
                           .then_inc(actS_ready, 1)

                    def first():
                        ln_stats_tile(dve, "a", 0, 0)
                        ln_stats_tile(dve, "a", 1, 1)
                        norm_a(0, 0)
                        dve.wait_ge(c3, 11)

                    def step(n, par, scores, values, routes, dispatch):
                        loop = not isinstance(n, int)
                        if dispatch:
                            places(n - 3, 1 - par)
                        if routes:
                            norm_b(n - 2, par)
                        if scores:
                            if loop or n + 1 < TILES:
                                norm_a(n + 1, 1 - par)
                            largest(n, par)
                        if routes:
                            route(n - 2, par)
                        if scores:
                            if loop or n + 2 < TILES:
                                stats_a(n + 2, par)
                            denominators(n, par)
                        if values:
                            add_values(n - 1, 1 - par)

                    steps_pipelined(dve, first, step, chain, 34)

                @block.tensor
                def _(pe):
                    def transpose_a(n, par):
                        pe.wait_ge(a_xn, n + 1)
                        want(pe, b_xT, n - 2)
                        want(pe, a_xT, n)
                        for k in range(KD):
                            last = pe.transpose(bank[:, 6, (KD + k) * P:(KD + k + 1) * P], xa[:, par, k * P:(k + 1) * P],
                                                ident[:])
                        last.then_inc(a_T, 1)

                    def first():
                        pe.wait_ge(w3_in, 48)
                        pe.wait_ge(c3, 11)
                        transpose_a(0, 0)

                    def score(n, par):
                        pe.wait_ge(wqk_in, 16 * (n // 8) + 16)
                        pe.wait_ge(a_xT, n + 1)
                        for a, (h, count) in enumerate(SPLIT):
                            want(pe, exp_done, 0 if isinstance(n, int) and n == 0 else 3 * n + (a - 2))
                            cols = slice(h * S, (h + count) * S)
                            to = bank[:, a, 0:count * S]
                            pe.matmul(to, onerow[0:1, :],
                                      mrow[0:1, bass.ds(n // 8, 1), cols].rearrange("p a n -> p (a n)"), start=True, stop=False)
                            for k in range(KD):
                                last = pe.matmul(to, xaT[:, par, k, :],
                                                 wqk[:, bass.ds((n // 8) % 2, 1), k, cols].rearrange("p a n -> p (a n)"),
                                                 start=False, stop=k == KD - 1)
                        last.then_inc(e_mm, 1)

                    def transpose_att(n, par, g):
                        if g == 0:
                            pe.wait_ge(att_ready, n + 1)
                        want(pe, at_out, 3 * n + (g - 1 if g != 1 else -1))
                        for j in range(4 * g, min(4 * g + 4, JC)):
                            w = min(P, HS - j * P)
                            last = pe.transpose(bank[0:w, 3 + g % 2, (j % 4) * P:(j % 4 + 1) * P],
                                                att[:, par, j * P:j * P + w], ident[:])
                        last.then_inc(at_T, 1)

                    def values_mm(n, par):
                        pe.wait_ge(vwo_in, 32 * (n // 8) + 32)
                        pe.wait_ge(at_out, 3 * n + 3)
                        want(pe, sd_added, n - 1)
                        want(pe, av_added, n)
                        for j in range(JC):
                            w = min(P, HS - j * P)
                            last = pe.matmul(bank[:, 5, 0:D], attT[0:w, par, j, :],
                                             vwo[0:w, bass.ds((n // 8) % 2, 1), j, :].rearrange("p a n -> p (a n)"),
                                             start=j == 0, stop=j == JC - 1)
                        last.then_inc(av_mm, 1)

                    def step(n, par, scores, values, routes, dispatch):
                        loop = not isinstance(n, int)
                        if dispatch:
                            m, mp = n - 3, 1 - par
                            pe.wait_ge(msel_ready, m + 1)
                            pe.wait_ge(actS_ready, m + 1)
                            pe.matmul(bank[:, 7, 288:288 + E1], tri[:], mselb[:, mp, :], start=True, stop=False)
                            pe.matmul(bank[:, 7, 288:288 + E1], allone[:], cum[:, mp, :], start=False, stop=True)\
                              .then_inc(pos_mm, 1)
                            pe.wait_ge(av_added, m + 2 if loop else min(m + 2, TILES))
                            pe.matmul(bank[:, 5, D:2 * D], actS[:, mp, :], sdn[:], start=True, stop=True).then_inc(sd_mm, 1)
                        if scores:
                            score(n, par)
                        if routes:
                            m = n - 2
                            pe.wait_ge(b_xn, m + 1)
                            pe.wait_ge(a_xT, n + 1 if loop else min(n + 1, TILES))
                            for k in range(KD):
                                last = pe.transpose(bank[:, 6, k * P:(k + 1) * P], rows[:, par, 0, k * P:(k + 1) * P], ident[:])
                            last.then_inc(b_T, 1)
                        if values:
                            transpose_att(n - 1, 1 - par, 0)
                            transpose_att(n - 1, 1 - par, 1)
                        if routes:
                            pe.wait_ge(b_xT, m + 1)
                            want(pe, pos_read, m)
                            for half in range(2):
                                for k in range(KD):
                                    last = pe.matmul(bank[:, 7, half * P:(half + 1) * P], sgu[:, k, half * P:(half + 1) * P],
                                                     xbT[:, par, k, :], start=k == 0, stop=k == KD - 1)
                            for k in range(KD):
                                last = pe.matmul(bank[:, 7, 256:256 + E1], xbT[:, par, k, :], wr1[:, k, :],
                                                 start=k == 0, stop=k == KD - 1)
                            last.then_inc(r_mm, 1)
                        if values:
                            transpose_att(n - 1, 1 - par, 2)
                        if scores and (loop or n + 1 < TILES):
                            transpose_a(n + 1, 1 - par)
                        if values:
                            values_mm(n - 1, 1 - par)

                    steps_pipelined(pe, first, step)

        four = ExitStack()
        with four:
            NB = 4
            BLK = CAP // P
            wgu = sb("expert_gate_up", [P, NB, KD, 2 * P], at=four)
            wd = sb("expert_down", [P, NB, D], at=four)
            xg = sb("expert_rows", [P, NB, BLK, ROW], at=four)
            target = sb("target_rows", [P, NB, BLK], I32, at=four)
            xgT = sb("expert_rowsT", [P, 2, KD, CAP], at=four)
            sgE = sb("expert_silu", [P, 2, CAP], at=four)
            hidT = sb("expert_hiddenT", [P, 2, CAP], at=four)
            y = sb("expert_out", [P, NB, BLK, D], at=four)
            in4 = [sem(f"expert_in{i}") for i in range(NB)]
            sent4 = [sem(f"expert_sent{i}") for i in range(NB)]
            g_T, g_xT, g_mm, g_silu, g_hid, g_down, g_y, targets = (
                sem("g_T"), sem("g_xT"), sem("g_mm"), sem("g_silu"), sem("g_hid"), sem("g_down"), sem("g_y"),
                sem("targets"))

            def experts_pipelined(eng, step_fn):
                def run(s):
                    step_fn(s, s % NB, s < E1, 1 <= s <= E1, s >= 2)
                for s in range(NB):
                    run(s)
                with eng.Fori(1, E1 // NB) as i:
                    for j in range(NB):
                        step_fn(NB * i + j, j, True, True, True)
                for s in range(E1, E1 + 2):
                    run(s)

            with nc.Block() as block:
                @block.sync
                def _(sp):
                    def load(e, j):
                        sp.dma_start(xg[:, j, :, :], slots_d.rearrange("(e b p) w -> e p b w", p=P, b=BLK)
                                     [bass.ds(e, 1), :, :, :].rearrange("a p b w -> p (a b) w")).then_inc(in4[j], 16)
                        sp.dma_start(wgu[:, j, :, :], io["wgu1"].rearrange("e (k p) n -> e p k n", p=P)
                                     [bass.ds(e, 1), :, :, :].rearrange("a p k n -> p (a k) n")).then_inc(in4[j], 16)
                        sp.dma_start(wd[:, j, :], io["wd1"][bass.ds(e, 1), :, :].rearrange("a p n -> p (a n)"))\
                          .then_inc(in4[j], 16)
                    for e in range(NB):
                        load(e, e)
                    with sp.Fori(1, E1 // NB) as i:
                        for j in range(NB):
                            e = NB * i + j
                            sp.wait_ge(targets, e - (NB - 1))
                            sp.wait_ge(g_down, e - (NB - 1))
                            load(e, j)

                @block.gpsimd
                def _(pool):
                    def send(e, j):
                        wait_apart(pool, g_y, e + 1, passed_pool)
                        for b in range(BLK):
                            pool.indirect_dma_start(
                                y_d, bass.IndirectOffsetOnAxis(ap=target[:, j, b:b + 1], axis=0),
                                y[:, j, b, :], None, bounds_check=T * K1 - 1, oob_is_err=False).then_inc(sent4[j], 16)
                    with pool.Fori(0, E1 // NB) as i:
                        for j in range(NB):
                            send(NB * i + j, j)
                    for j in range(NB):
                        pool.wait_ge(sent4[j], 16 * BLK * (E1 // NB))

                @block.scalar
                def _(act):
                    def step(s, j, transposed, hidden, output):
                        if hidden:
                            act.wait_ge(g_mm, s)
                            want(act, g_hid, s - 2)
                            act.activation(sgE[:, (j + 1) % 2, :], bank[:, 2 + (j + 1) % 2, 0:CAP], ACT.Silu)\
                               .then_inc(g_silu, 1)
                        if transposed:
                            act.wait_ge(g_T, s + 1)
                            want(act, g_mm, s - 1)
                            act.activation(xgT[:, j % 2, :, :].rearrange("p k t -> p (k t)"), bank[:, j % 2, :],
                                           ACT.Copy).then_inc(g_xT, 1)

                    experts_pipelined(act, step)

                @block.vector
                def _(dve):
                    def step(s, j, transposed, hidden, output):
                        if transposed:
                            loop = not isinstance(s, int)
                            dve.wait_ge(in4[j], 48 * (s // NB) + 48 if loop else 48)
                            want(dve, sent4[j], 16 * BLK * (s // NB))
                            dve.tensor_copy(target[:, j, :], xg[:, j, :, D:D + 1].bitcast(I32)
                                            .rearrange("p b a -> p (b a)")).then_inc(targets, 1)
                        if hidden:
                            dve.wait_ge(g_silu, s)
                            want(dve, g_down, s - 2)
                            dve.tensor_tensor(hidT[:, (j + 1) % 2, :], sgE[:, (j + 1) % 2, :],
                                              bank[:, 2 + (j + 1) % 2, CAP:2 * CAP], ALU.mult).then_inc(g_hid, 1)
                        if output:
                            m = (j + 2) % NB
                            dve.wait_ge(g_down, s - 1)
                            want(dve, sent4[m], 16 * BLK * ((s - 2) // NB))
                            dve.tensor_copy(y[:, m, :, :].rearrange("p b n -> p (b n)"), bank[:, 4 + j % 2, :])\
                               .then_inc(g_y, 1)

                    experts_pipelined(dve, step)

                @block.tensor
                def _(pe):
                    def step(s, j, transposed, hidden, output):
                        if transposed:
                            pe.wait_ge(in4[j], 48 * (s // NB) + 48)
                            pe.wait_ge(targets, s + 1)
                            want(pe, g_xT, s - 1)
                            for b in range(BLK):
                                for k in range(KD):
                                    last = pe.transpose(bank[:, j % 2, k * CAP + b * P:k * CAP + (b + 1) * P],
                                                        xg[:, j, b, k * P:(k + 1) * P], ident[:])
                            last.then_inc(g_T, 1)
                        if hidden:
                            q, m = (j + 1) % 2, (j + NB - 1) % NB
                            pe.wait_ge(g_xT, s)
                            want(pe, g_hid, s - 2)
                            for half in range(2):
                                for k in range(KD):
                                    last = pe.matmul(bank[:, 2 + q, half * CAP:(half + 1) * CAP],
                                                     wgu[:, m, k, half * P:(half + 1) * P], xgT[:, q, k, :],
                                                     start=k == 0, stop=k == KD - 1)
                            last.then_inc(g_mm, 1)
                        if output:
                            q, m = j % 2, (j + 2) % NB
                            pe.wait_ge(g_hid, s - 1)
                            want(pe, g_y, s - 3)
                            for b in range(BLK):
                                last = pe.matmul(bank[:, 4 + q, b * D:(b + 1) * D], hidT[:, q, b * P:(b + 1) * P],
                                                 wd[:, m, :], start=True, stop=True)
                            last.then_inc(g_down, 1)

                    experts_pipelined(pe, step)

        five = ExitStack()
        with five:
            yk = sb("choice_rows", [P, 3, CT, K1, D], at=five)
            yk_in = [sem(f"yk_in{i}") for i in range(3)]
            summed, done_out, d5 = sem("summed"), sem("done_out"), sem("dve_steps_5")
            with nc.Block() as block:
                @block.sync
                def _(sp):
                    for c in range(CHUNKS):
                        want(sp, summed, CT * (c - 2))
                        sp.dma_start(yk[:, c % 3, :, :, :], y_d.rearrange("(n p k) d -> p n k d", p=P, k=K1)
                                     [:, c * CT:(c + 1) * CT, :, :]).then_inc(yk_in[c % 3], 16)
                    sp.wait_ge(done_out, 16 * CHUNKS)

                @block.scalar
                def _(act):
                    for c in range(CHUNKS):
                        act.wait_ge(summed, CT * (c + 1))
                        act.dma_start(out_v[:, c * CT:(c + 1) * CT, :], x[:, c * CT:(c + 1) * CT, :]).then_inc(done_out, 16)

                @block.vector
                def _(dve):
                    step = Chain(dve, d5, passed)
                    for c in range(CHUNKS):
                        dve.wait_ge(yk_in[c % 3], 16 * (c // 3 + 1))
                        for k in range(K1):
                            for t in range(CT):
                                row = x[:, c * CT + t, :]
                                last = dve.scalar_tensor_tensor(row, yk[:, c % 3, t, k, :], wk[:, c * CT + t, k:k + 1], row,
                                                                ALU.mult, ALU.add)
                                if k == K1 - 1:
                                    last.then_inc(summed, 1)
                            if k < K1 - 1:
                                step(last)



def hilbert_table():
    f = np.arange(L)
    weight = np.where((f == 0) | (f == L // 2), 1.0, 2.0)[:L // 2 + 1]
    angle = 2 * np.pi / L
    full = np.cos(angle * (np.outer(np.arange(L), f[:L // 2 + 1]) % L)) * weight
    table = full @ np.sin(angle * (np.outer(f[:L // 2 + 1], np.arange(CHUNK)) % L))
    return (table / (2 * L * D)).astype(np.float32)


def kernel(**inputs):
    import concourse.bacc as bacc
    from concourse.bass_utils import run_bass_kernel_spmd

    a = {k: np.asarray(v) for k, v in inputs.items()}
    flip = a["ctx_1024"][:, ::-1, :]
    gu = a["L0_ffn_gate_up_proj"].transpose(2, 0, 1)
    sg = a["L0_ffn_shared_gate_w"].T.reshape(D, 4, 1, P)
    su = a["L0_ffn_shared_up_w"].T.reshape(D, 4, 1, P)
    arrays = {
        "x": a["x"].reshape(T, D),
        "ctxT": flip.reshape(BS, D).T,
        "mask": a["mask_BxS2_bk0"][:, ::-1],
        "g_xattn": a["g_xattn"], "g_ffn": a["g_ffn"],
        "wk0": a["L0_xattn_Wk"], "wqT0": a["L0_xattn_Wq"].T, "wv0": a["L0_xattn_Wv"], "wo0": a["L0_xattn_Wo"],
        "bias0": np.stack([a["L0_xattn_bq"], a["L0_xattn_bk"], a["L0_xattn_bv"]]).reshape(3, KD, P)
                   .transpose(2, 0, 1).reshape(P, 3 * KD),
        "bo0": a["L0_xattn_bo"],
        "htab": hilbert_table(),
        "wgu0": np.concatenate([gu.reshape(D, E0 * 2 * P),
                                np.concatenate([sg, su], 2).reshape(D, 4 * 2 * P)], 1),
        "wd0": np.concatenate([a["L0_ffn_down_proj"].transpose(0, 2, 1).reshape(E0 * P, D),
                               a["L0_ffn_shared_down_w"].T], 0),
        "wr0": np.concatenate([a["L0_ffn_router_weight"]] + 2 * [a["L0_ffn_shared_expert_gate_w"]], 0).T,
        "wk1": a["L1_xattn_W_K"], "wv1": a["L1_xattn_W_V"], "wqT1": a["L1_xattn_W_Q"].T, "wo1": a["L1_xattn_W_O"],
        "wr1": a["L1_ffn_gate_w"].T,
        "wgu1": a["L1_ffn_w_gate_up"], "wd1": a["L1_ffn_w_down"],
        "sgu1": a["L1_ffn_shared_w_gate_up"], "sd1": a["L1_ffn_shared_w_down"],
    }
    arrays = {k: np.ascontiguousarray(v) for k, v in arrays.items()}
    nc = bacc.Bacc("TRN2", target_bir_lowering=False, num_devices=1)
    io = {k: nc.dram_tensor(f"in_{k}", v.shape, mybir.dt.from_np(v.dtype), kind="ExternalInput").ap()
          for k, v in arrays.items()}
    io["out"] = nc.dram_tensor("result", (T, D), F32, kind="ExternalOutput").ap()
    build(nc, io)
    r = run_bass_kernel_spmd(nc, [{f"in_{k}": v for k, v in arrays.items()}], core_ids=[0])
    return r.results[0]["result"].reshape(B, L, D)
```

```python
from contextlib import ExitStack

import numpy as np

import concourse.bass as bass
from concourse import mybir

ALU = mybir.AluOpType
ACT = mybir.ActivationFunctionType
AX = mybir.AxisListType
F32 = mybir.dt.float32
BF16 = mybir.dt.bfloat16
I32 = mybir.dt.int32
F32R = mybir.dt.float32r

P = 128
B, L, D = 4, 1024, 256
S = 77
T = B * L
TILES = T // P
CHUNK = 512
CT = CHUNK // P
CHUNKS = T // CHUNK
KD = D // P
BS = B * S
TOPK = 13
WROW = L + S - 1
E0, UNITS = 8, 12
R0 = E0 + 2
H1, DK = 16, 64
HS = H1 * S
EPS = 1e-5
E1, K1, CAP = 32, 4, 256
SLOTS = E1 * CAP
ROW = 260
NEG = -3.0e38
SENTINEL = 3.3e38
MASKED = -1.0e30
FAR = 1.0e6


def want(eng, sem, value):
    if isinstance(value, int) and value <= 0:
        return
    eng.wait_ge(sem, value)


def wait_apart(eng, sem, value, passed):
    if isinstance(value, int):
        want(eng, sem, value)
    else:
        eng.wait_ge(sem, value)
        eng.sem_inc(passed, 1)


class Chain:

    def __init__(self, eng, sem, passed):
        self.passed = passed
        self.eng, self.sem, self.base, self.i, self.local = eng, sem, 0, None, 0

    def enter(self, i, per):
        self.i, self.per, self.local = i, per, 0

    def leave(self, rounds):
        assert self.local == self.per, ("steps of a round", self.local)
        self.base += self.per * rounds
        self.i = None
        self.local = 0

    def mark(self, ins):
        ins.then_inc(self.sem, 1)
        if self.i is None:
            self.base += 1
            return self.base
        self.local += 1
        return self.per * self.i + (self.base + self.local)

    def need(self, count):
        wait_apart(self.eng, self.sem, count, self.passed)

    def __call__(self, ins):
        self.need(self.mark(ins))


def build(nc, io):
    root = ExitStack()
    with root:
        def sem(name):
            return root.enter_context(nc.semaphore(name))

        def sb(name, shape, dt=F32, at=root):
            return at.enter_context(nc.sbuf_tensor(name, shape, dt))

        bank = root.enter_context(nc.psum_tensor("bank", [P, 8, 512], F32))

        x = sb("x_res", [P, TILES, D])
        ident = sb("ident", [P, P])
        gates = sb("gates", [P, 4])
        tg = sb("tanh_gates", [P, 4])
        neghalf = sb("neghalf", [P, CT])
        mrow = sb("mask_row", [1, B, S], BF16)
        onerow = sb("onerow", [1, P], BF16)
        wk = sb("wk", [P, TILES, K1])
        early = root.enter_context(ExitStack())
        wgu0 = sb("wgu0", [P, KD, UNITS * 2 * P], at=early)
        wd0 = sb("wd0", [P, UNITS, D], at=early)
        wr0 = sb("wr0", [P, KD, R0], at=early)
        vwo0 = sb("vwo0", [S + 1, B, D], at=early)
        bst = sb("bst", [P, 2, CT, 6], at=early)
        mv = sb("mv", [P, 2, CT, 2], at=early)
        veps = sb("veps", [P, 2, CT], at=early)
        rstd = sb("rstd", [P, 2, CT], at=early)
        xn = sb("xn", [P, 2, CT, D], at=early)

        passed, passed_pool, passed_pe = sem("passed"), sem("passed_pool"), sem("passed_pe")
        x_in = [sem(f"x_in{c}") for c in range(CHUNKS)]
        ident_zero, ident_ready, consts_ready = sem("ident_zero"), sem("ident_ready"), sem("consts_ready")
        gates_in, tg_ready = sem("gates_in"), sem("tg_ready")
        ffn0_w_in = sem("ffn0_w_in")
        ln_bst, ln_stats, ln_veps, ln_rstd = sem("ln_bst"), sem("ln_stats"), sem("ln_veps"), sem("ln_rstd")
        ln_xn, ln_T, ln_xT = sem("ln_xn"), sem("ln_T"), sem("ln_xT")

        st_d = nc.dram_tensor("st_d", (B, S, 2 * L), F32, kind="Internal").ap()
        w_d = nc.dram_tensor("w_d", (B, WROW), F32, kind="Internal").ap()
        wqk_d = nc.dram_tensor("wqk_d", (B, D, HS), F32, kind="Internal").ap()
        vwo_d = nc.dram_tensor("vwo_d", (B, HS, D), F32, kind="Internal").ap()
        slots_d = nc.dram_tensor("slots_d", (SLOTS, ROW), F32, kind="Internal").ap()
        y_d = nc.dram_tensor("y_d", (T * K1, D), F32, kind="Internal").ap()

        out = io["out"]
        x_v = io["x"].rearrange("(n p) d -> p n d", p=P)
        out_v = out.rearrange("(n p) d -> p n d", p=P)

        def ln_stats_job(dve, q, c, par):
            wait_apart(dve, ln_xn, 4 * (q - 1), passed)
            tile0 = c * CT
            for t in range(CT):
                dve.bn_stats(bst[:, par, t, :], x[:, bass.ds(tile0 + t, 1), :]).then_inc(ln_bst, 1)
            for t in range(CT):
                wait_apart(dve, ln_bst, 4 * q + (t + 1), passed)
                dve.bn_aggr(mv[:, par, t, :], bst[:, par, t, :]).then_inc(ln_stats, 1)

        def ln_rstd_job(pool, q, par):
            wait_apart(pool, ln_stats, 4 * q + 4, passed_pool)
            pool.tensor_scalar_add(veps[:, par, :], mv[:, par, :, 1], EPS).then_inc(ln_veps, 1)
            pool.wait_ge(ln_veps, 1 * q + 1)
            pool.tensor_tensor(rstd[:, par, :], veps[:, par, :], neghalf[:, 0:CT], ALU.pow).then_inc(ln_rstd, 1)

        def ln_norm_job(dve, q, c, par):
            dve.wait_ge(ln_rstd, q + 1)
            want(dve, ln_T, q - 1)
            tile0 = c * CT
            for t in range(CT):
                dve.tensor_scalar(xn[:, par, t, :], x[:, bass.ds(tile0 + t, 1), :], mv[:, par, t, 0:1],
                                  rstd[:, par, t:t + 1], ALU.subtract, ALU.mult).then_inc(ln_xn, 1)

        def ln_transpose_job(pe, q, par):
            pe.wait_ge(ln_xn, 4 * q + 4)
            want(pe, ln_xT, 2 * q)
            for t in range(CT):
                for k in range(KD):
                    last = pe.transpose(bank[:, k, t * P:(t + 1) * P], xn[:, par, t, k * P:(k + 1) * P], ident[:])
            last.then_inc(ln_T, 1)

        def ln_evict_job(act, q, par):
            act.wait_ge(ln_T, q + 1)
            for k in range(KD):
                act.activation(xnT[:, par, k, :], bank[:, k, :], ACT.Copy).then_inc(ln_xT, 1)

        one = ExitStack()
        with one:
            xnT = sb("xnT", [P, 2, KD, CHUNK], at=one)
            ctxT = sb("ctxT", [P, KD, BS], at=one)
            wk0 = sb("wk0", [P, KD, D], at=one)
            wqT0 = sb("wqT0", [P, KD, D], at=one)
            wv0 = sb("wv0", [P, KD, D], at=one)
            wo0 = sb("wo0", [P, KD, D], at=one)
            bias0 = sb("bias0", [P, 3, KD], at=one)
            kT0 = sb("kT0", [P, KD, BS], at=one)
            vT0 = sb("vT0", [P, KD, BS], at=one)
            wqk0 = sb("wqk0", [P, KD, BS], at=one)
            bqk = sb("bqk", [S, B], at=one)
            sT = sb("sT", [S, 2, CHUNK], at=one)
            skew = sb("skew", [S, 2, 2, L], at=one)
            signs = sb("signs", [S, 4], at=one)
            sumU = sb("sumU", [P, 8, B], at=one)
            difV = sb("difV", [P, 8, B], at=one)
            htab = sb("htab", [P, 8, CHUNK], at=one)
            urow = sb("urow", [B, L + 1], at=one)
            even = sb("even", [B, L], at=one)
            mean = sb("mean", [B, L], at=one)
            top = sb("top", [B, 16], at=one)
            left1 = sb("left1", [B, L], at=one)
            negmax = sb("negmax", [B, 1], at=one)
            expm = urow[:, 0:L]
            wsel = even
            wsum = sb("wsum", [B, 2], at=one)
            wrow = sb("wrow", [B, WROW], at=one)
            left2 = wrow[:, 0:L]
            NH = 3
            wk1 = sb("wk1", [P, NH, KD, P], at=one)
            wv1 = sb("wv1", [P, NH, KD, P], at=one)
            wqT1 = sb("wqT1", [P, NH, D], at=one)
            wo1 = sb("wo1", [P, NH, D], at=one)
            kT1 = sb("kT1", [P, 2, BS], at=one)
            vT1 = sb("vT1", [P, 2, BS], at=one)
            wqk1 = sb("wqk1", [P, 2, KD, B, 2 * S], at=one)
            vwo1 = sb("vwo1", [S, 2, 2, B, D], at=one)

            w0_in, htab_in, bo_in = sem("w0_in"), sem("htab_in"), sem("bo_in")
            fold_mm, kT0_ready, vT0_ready = sem("fold_mm"), sem("kT0_ready"), sem("vT0_ready")
            fold_out, vwo_mm, vwo_out = sem("fold_out"), sem("vwo_mm"), sem("vwo_out")
            s_mm, s_out, s_stored = sem("s_mm"), sem("s_out"), [sem("s_stored0"), sem("s_stored1")]
            skew_in, uv_mm, uv_out = [sem("skew_in0"), sem("skew_in1")], sem("uv_mm"), sem("uv_out")
            h_mm, ex_ready, nm_ready, w_ready, w_stored = (sem("h_mm"), sem("ex_ready"), sem("nm_ready"),
                                                           sem("w_ready"), sem("w_stored"))
            w1_in = [sem(f"w1_in{i}") for i in range(NH)]
            kv1_mm, k1_out, v1_out = sem("kv1_mm"), sem("k1_out"), sem("v1_out")
            f1_mm, f1_out = sem("fold1_mm"), sem("fold1_out")
            qk1_stored, vo1_stored = ([sem("qk1_stored0"), sem("qk1_stored1")],
                                      [sem("vo1_stored0"), sem("vo1_stored1")])
            d1 = sem("dve_steps_1")

            with nc.Block() as block:
                @block.sync
                def _(sp):
                    for name, dst in (("ctxT", ctxT), ("wk0", wk0), ("wqT0", wqT0), ("wv0", wv0), ("wo0", wo0)):
                        sp.dma_start(dst[:], io[name].rearrange("(k p) n -> p k n", p=P)).then_inc(w0_in, 16)
                    sp.dma_start(bias0[:], io["bias0"].rearrange("p (a k) -> p a k", a=3)).then_inc(w0_in, 16)
                    for c in range(CHUNKS):
                        sp.dma_start(x[:, c * CT:(c + 1) * CT, :], x_v[:, c * CT:(c + 1) * CT, :]).then_inc(x_in[c], 16)
                    for b in range(B):
                        sp.dma_start(vwo0[S:S + 1, b, :], io["bo0"].rearrange("(a n) -> a n", a=1)).then_inc(bo_in, 16)
                    sp.dma_start(htab[:], io["htab"].rearrange("(c p) n -> p c n", p=P)).then_inc(htab_in, 16)
                    for c in range(CHUNKS):
                        b, half = c // 2, c % 2
                        sp.wait_ge(s_out, c + 1)
                        for copy in range(2):
                            sp.dma_start(st_d[b, :, copy * L + half * CHUNK:copy * L + (half + 1) * CHUNK],
                                         sT[:, half, :]).then_inc(s_stored[half], 16)
                        if half:
                            for par in range(2):
                                sp.wait_ge(s_stored[par], 32 * (b + 1))
                            want(sp, uv_mm, b - 1)
                            for sign in range(2):
                                shift = bass.AP(st_d.tensor, b * S * 2 * L + (S - 1 if sign == 0 else L - S + 1),
                                                [[2 * L - 1 if sign == 0 else 2 * L + 1, S], [1, L]])
                                sp.dma_start(skew[:, b % 2, sign, :], shift).then_inc(skew_in[b % 2], 16)
                    sp.wait_ge(w_ready, 2)
                    sp.dma_start(w_d, wrow[:]).then_inc(w_stored, 16)
                    sp.wait_ge(w_stored, 16)

                @block.gpsimd
                def _(pool):
                    pool.memset(ident[:], 0.0).then_inc(ident_zero, 1)
                    pool.memset(neghalf[:], -0.5).then_inc(consts_ready, 1)
                    pool.memset(signs[:, 0:3], 1.0).then_inc(consts_ready, 1)
                    pool.memset(signs[:, 3:4], -1.0).then_inc(consts_ready, 1)
                    pool.wait_ge(ident_zero, 1)
                    pool.affine_select(out=ident[:], in_=ident[:], compare_op=ALU.not_equal, fill=1.0, base=0,
                                       pattern=[[-1, P]], channel_multiplier=1).then_inc(ident_ready, 1)
                    pool.wait_ge(consts_ready, 3)
                    for c in range(CHUNKS):
                        ln_rstd_job(pool, c, c % 2)

                @block.scalar
                def _(act):
                    act.dma_start(gates[:, 0:2], bass.AP(io["g_xattn"].tensor, 0, [[0, P], [1, 2]])).then_inc(gates_in, 16)
                    act.dma_start(gates[:, 2:4], bass.AP(io["g_ffn"].tensor, 0, [[0, P], [1, 2]])).then_inc(gates_in, 16)
                    act.wait_ge(gates_in, 32)
                    act.activation(tg[:], gates[:], ACT.Tanh).then_inc(tg_ready, 1)

                    def load_heads(m):
                        want(act, f1_mm, 8 * (m - NH + 1))
                        cols = slice(m * P, (m + 1) * P)
                        for w, src in ((wk1, "wk1"), (wv1, "wv1")):
                            act.dma_start(w[:, m % NH, :, :], io[src].rearrange("(k p) n -> p k n", p=P)[:, :, cols])\
                               .then_inc(w1_in[m % NH], 16)
                        for w, src in ((wqT1, "wqT1"), (wo1, "wo1")):
                            act.dma_start(w[:, m % NH, :], io[src][cols, :]).then_inc(w1_in[m % NH], 16)

                    def store_heads(m):
                        act.wait_ge(f1_out, 8 * m + 4)
                        for b in range(B):
                            act.dma_start(wqk_d[b].rearrange("(k p) n -> p k n", p=P)[:, :, 2 * m * S:2 * (m + 1) * S],
                                          wqk1[:, m % 2, :, b, :]).then_inc(qk1_stored[m % 2], 16)
                        act.wait_ge(f1_out, 8 * m + 8)
                        for hh in range(2):
                            h = 2 * m + hh
                            act.dma_start(vwo_d[:, h * S:(h + 1) * S, :].rearrange("b s n -> s b n"),
                                          vwo1[:, m % 2, hh, :, :]).then_inc(vo1_stored[m % 2], 16)

                    for m in range(NH):
                        load_heads(m)
                    act.dma_start(wgu0[:], io["wgu0"].rearrange("(k p) n -> p k n", p=P)).then_inc(ffn0_w_in, 16)
                    act.dma_start(wd0[:], io["wd0"].rearrange("(u p) n -> p u n", p=P)).then_inc(ffn0_w_in, 16)
                    act.dma_start(wr0[:], io["wr0"].rearrange("(k p) n -> p k n", p=P)).then_inc(ffn0_w_in, 16)
                    act.wait_ge(w0_in, 96)
                    for m in range(KD):
                        act.wait_ge(fold_mm, m + 1)
                        act.activation(kT0[:, m, :], bank[:, m, 0:BS], ACT.Identity, bias=bias0[:, 1, m:m + 1])\
                           .then_inc(kT0_ready, 1)
                    for m in range(KD):
                        act.wait_ge(fold_mm, KD + m + 1)
                        act.activation(vT0[:, m, :], bank[:, 2 + m, 0:BS], ACT.Identity, bias=bias0[:, 2, m:m + 1])\
                           .then_inc(vT0_ready, 1)
                    act.wait_ge(fold_out, 3)

                    def scores(c):
                        if c + 1 < CHUNKS:
                            want(act, s_mm, c)
                            ln_evict_job(act, c + 1, (c + 1) % 2)
                        act.wait_ge(s_mm, c + 1)
                        want(act, s_stored[c % 2], 32 * (c // 2))
                        act.activation(sT[:, c % 2, :], bank[0:S, 2, :], ACT.Identity,
                                       bias=bqk[:, c // 2:c // 2 + 1]).then_inc(s_out, 1)

                    def keys_values(m):
                        act.wait_ge(kv1_mm, 2 * m + 1)
                        want(act, f1_mm, 8 * (m - 1))
                        act.activation(kT1[:, m % 2, :], bank[:, 4, 0:BS], ACT.Copy, scale=DK ** -0.5).then_inc(k1_out, 1)
                        act.wait_ge(kv1_mm, 2 * m + 2)
                        act.activation(vT1[:, m % 2, :], bank[:, 5, 0:BS], ACT.Copy).then_inc(v1_out, 1)

                    def fold_heads(m):
                        want(act, qk1_stored[m % 2], 16 * B * (m // 2))
                        want(act, vo1_stored[m % 2], 16 * 2 * (m // 2))
                        for n in range(8):
                            hh, i = n // 2 % 2, n % 2
                            act.wait_ge(f1_mm, 8 * m + n + 1)
                            if n < 4:
                                act.activation(wqk1[:, m % 2, i, :, hh * S:(hh + 1) * S],
                                               bank[:, 6 + i, 0:BS].rearrange("p (b s) -> p b s", b=B), ACT.Copy)\
                                   .then_inc(f1_out, 1)
                            else:
                                act.activation(vwo1[:, m % 2, hh, 2 * i:2 * i + 2, :],
                                               bank[0:S, 6 + i, :].rearrange("p (b n) -> p b n", b=2), ACT.Copy,
                                               scale=tg[0:S, 1:2]).then_inc(f1_out, 1)
                        store_heads(m)
                        if m + NH < CHUNKS:
                            load_heads(m + NH)

                    ln_evict_job(act, 0, 0)
                    keys_values(0)
                    for c in range(CHUNKS):
                        scores(c)
                        if c % 2:
                            keys_values((c + 1) // 2)
                            fold_heads(c // 2)
                    for m in range(CHUNKS // 2, CHUNKS):
                        if m + 1 < CHUNKS:
                            keys_values(m + 1)
                        fold_heads(m)
                        if m == CHUNKS - 2:
                            act.wait_ge(nm_ready, 1)
                            act.activation(expm, mean[:], ACT.Exp, bias=negmax[:, 0:1]).then_inc(ex_ready, 1)
                    for par in range(2):
                        act.wait_ge(qk1_stored[par], 16 * B * 4)
                        act.wait_ge(vo1_stored[par], 16 * 2 * 4)
                    act.wait_ge(ffn0_w_in, 48)

                @block.vector
                def _(dve):
                    step = Chain(dve, d1, passed)
                    for m in range(KD):
                        dve.wait_ge(fold_mm, 2 * KD + m + 1)
                        dve.tensor_copy(wqk0[:, m, :], bank[:, 4 + m, 0:BS]).then_inc(fold_out, 1)
                    dve.wait_ge(fold_mm, 3 * KD + 1)
                    dve.tensor_copy(bqk[:], bank[0:S, 6, 0:B]).then_inc(fold_out, 1)
                    for b in range(B):
                        dve.wait_ge(vwo_mm, b + 1)
                        dve.tensor_copy(vwo0[0:S, b, :], bank[0:S, 4 + b, 0:D]).then_inc(vwo_out, 1)
                    dve.wait_ge(tg_ready, 1)

                    for c in range(2):
                        dve.wait_ge(x_in[c], 16)
                        ln_stats_job(dve, c, c, c % 2)
                        ln_norm_job(dve, c, c, c % 2)
                    for c in range(CHUNKS):
                        if c + 2 < CHUNKS:
                            dve.wait_ge(x_in[c + 2], 16)
                            ln_stats_job(dve, c + 2, c + 2, c % 2)
                            ln_norm_job(dve, c + 2, c + 2, c % 2)
                    dve.wait_ge(bo_in, 64)
                    dve.wait_ge(vwo_out, B)
                    dve.tensor_scalar(vwo0[:], vwo0[:], tg[0:S + 1, 0:1], None, ALU.mult).then_inc(vwo_out, 1)
                    dve.wait_ge(uv_mm, B)
                    uv = bank[:, 3, 0:B * 16].rearrange("p (b c u) -> p c b u", b=B, u=2)
                    dve.tensor_copy(sumU[:], uv[:, :, :, 0]).then_inc(uv_out, 1)
                    dve.tensor_copy(difV[:], uv[:, :, :, 1]).then_inc(uv_out, 1)
                    dve.wait_ge(h_mm, 1)
                    step(dve.tensor_copy(urow[:, 0:L], bank[0:B, 0:2, :].rearrange("p a n -> p (a n)")))
                    step(dve.tensor_copy(urow[:, L:L + 1], urow[:, 0:1]))
                    step(dve.tensor_tensor(even[:], urow[:, 0:L], urow[:, L:0:-1], ALU.add))
                    odd = bank[0:B, 2, :]
                    c4 = 1.0 / (4 * D)
                    step(dve.scalar_tensor_tensor(mean[:, 0:CHUNK], even[:, 0:CHUNK], c4, odd, ALU.mult, ALU.add))
                    step(dve.tensor_scalar(mean[:, CHUNK:CHUNK + 1], even[:, CHUNK:CHUNK + 1], c4, None, ALU.mult))
                    step(dve.scalar_tensor_tensor(mean[:, CHUNK + 1:L], even[:, CHUNK + 1:L], c4,
                                                  odd[:, CHUNK - 1:0:-1], ALU.mult, ALU.subtract))
                    step(dve.max(top[:, 0:8], mean[:]))
                    step(dve.match_replace(left1[:], top[:, 0:8], mean[:], NEG))
                    step(dve.max(top[:, 8:16], left1[:]))
                    step(dve.memset(top[:, TOPK:16], SENTINEL))
                    step(dve.match_replace(left2, top[:, 8:16], left1[:], NEG))
                    dve.tensor_scalar(negmax[:], top[:, 0:1], -1.0, None, ALU.mult).then_inc(nm_ready, 1)
                    dve.wait_ge(ex_ready, 1)
                    step(dve.scalar_tensor_tensor(wsel[:], left2, NEG, expm, ALU.is_equal, ALU.mult,
                                                  accum_out=wsum[:, 0:1]))
                    step(dve.reciprocal(wsum[:, 1:2], wsum[:, 0:1]))
                    dve.tensor_scalar(wrow[:, 0:S], wsel[:, S - 1::-1], wsum[:, 1:2], None, ALU.mult).then_inc(w_ready, 1)
                    dve.tensor_scalar(wrow[:, S:WROW], wsel[:, L - 1:0:-1], wsum[:, 1:2], None, ALU.mult)\
                       .then_inc(w_ready, 1)

                @block.tensor
                def _(pe):
                    pe.wait_ge(w0_in, 96)
                    for base, w in ((0, wk0), (2, wv0)):
                        for m in range(KD):
                            for k in range(KD):
                                last = pe.matmul(bank[:, base + m, 0:BS], w[:, k, m * P:(m + 1) * P], ctxT[:, k, :],
                                                 start=k == 0, stop=k == KD - 1)
                            last.then_inc(fold_mm, 1)
                    pe.wait_ge(kT0_ready, KD)
                    for m in range(KD):
                        for k in range(KD):
                            last = pe.matmul(bank[:, 4 + m, 0:BS], wqT0[:, k, m * P:(m + 1) * P], kT0[:, k, :],
                                             start=k == 0, stop=k == KD - 1)
                        last.then_inc(fold_mm, 1)
                    for b in range(B):
                        for k in range(KD):
                            last = pe.matmul(bank[0:S, 6, b:b + 1], kT0[:, k, b * S:(b + 1) * S], bias0[:, 0, k:k + 1],
                                             start=k == 0, stop=k == KD - 1)
                    last.then_inc(fold_mm, 1)
                    pe.wait_ge(vT0_ready, KD)
                    pe.wait_ge(fold_out, 3)
                    for b in range(B):
                        for k in range(KD):
                            last = pe.matmul(bank[0:S, 4 + b, 0:D], vT0[:, k, b * S:(b + 1) * S], wo0[:, k, :],
                                             start=k == 0, stop=k == KD - 1)
                        last.then_inc(vwo_mm, 1)
                    pe.wait_ge(ident_ready, 1)
                    pe.wait_ge(consts_ready, 3)

                    def scores(c):
                        pe.wait_ge(ln_xT, 2 * c + 2)
                        want(pe, s_out, c)
                        for k in range(KD):
                            last = pe.matmul(bank[0:S, 2, :], wqk0[:, k, (c // 2) * S:(c // 2 + 1) * S],
                                             xnT[:, c % 2, k, :], start=k == 0, stop=k == KD - 1)
                        last.then_inc(s_mm, 1)

                    def keys_values(m):
                        pe.wait_ge(w1_in[m % NH], 64 * (m // NH + 1))
                        for n, (w, done) in enumerate(((wk1, k1_out), (wv1, v1_out))):
                            want(pe, done, m)
                            for k in range(KD):
                                last = pe.matmul(bank[:, 4 + n, 0:BS], w[:, m % NH, k, :], ctxT[:, k, :],
                                                 start=k == 0, stop=k == KD - 1)
                            last.then_inc(kv1_mm, 1)

                    def fold_heads(m):
                        pe.wait_ge(k1_out, m + 1)
                        pe.wait_ge(v1_out, m + 1)
                        for n in range(8):
                            hh, i = n // 2 % 2, n % 2
                            rows = slice(hh * DK, (hh + 1) * DK)
                            want(pe, f1_out, 8 * m + n - 1)
                            if n < 4:
                                last = pe.matmul(bank[:, 6 + i, 0:BS], wqT1[rows, m % NH, i * P:(i + 1) * P],
                                                 kT1[rows, m % 2, :], start=True, stop=True)
                            else:
                                for b in range(2 * i, 2 * i + 2):
                                    last = pe.matmul(bank[0:S, 6 + i, (b % 2) * D:(b % 2 + 1) * D],
                                                     vT1[rows, m % 2, b * S:(b + 1) * S], wo1[rows, m % NH, :],
                                                     start=True, stop=True)
                            last.then_inc(f1_mm, 1)

                    def delay_sums(b):
                        pe.wait_ge(skew_in[b % 2], 32 * (b // 2 + 1))
                        for c in range(8):
                            for sign in range(2):
                                last = pe.matmul(bank[:, 3, (b * 8 + c) * 2:(b * 8 + c) * 2 + 2],
                                                 skew[:, b % 2, sign, c * P:(c + 1) * P],
                                                 signs[0:S, 2 * sign:2 * sign + 2], start=sign == 0, stop=sign == 1)
                        last.then_inc(uv_mm, 1)

                    def correlation():
                        pe.wait_ge(uv_out, 2)
                        pe.wait_ge(htab_in, 16)
                        pe.wait_ge(s_out, CHUNKS)
                        for c in range(8):
                            pe.matmul(bank[0:B, 2, :], difV[:, c, :], htab[:, c, :], start=c == 0, stop=c == 7)
                        pe.wait_ge(ln_xT, 2 * CHUNKS)
                        for c in range(8):
                            last = pe.transpose(bank[0:B, c // 4, (c % 4) * P:(c % 4 + 1) * P], sumU[:, c, :], ident[:])
                        last.then_inc(h_mm, 1)

                    ln_transpose_job(pe, 0, 0)
                    pe.wait_ge(vwo_out, B)
                    keys_values(0)
                    for c in range(CHUNKS):
                        if c + 1 < CHUNKS:
                            ln_transpose_job(pe, c + 1, (c + 1) % 2)
                        scores(c)
                        if c % 2:
                            keys_values((c + 1) // 2)
                            fold_heads(c // 2)
                            if c >= 5:
                                delay_sums((c - 5) // 2)
                    for m in range(CHUNKS // 2, CHUNKS):
                        if m + 1 < CHUNKS:
                            keys_values(m + 1)
                        fold_heads(m)
                        if m == CHUNKS // 2:
                            delay_sums(B - 2)
                            delay_sums(B - 1)
                        if m == CHUNKS // 2 + 1:
                            correlation()

        two = ExitStack()
        with two:
            mt = sb("shift_mt", [S + 1, 2, CHUNK], at=two)
            sg = sb("silu_gate", [P, 2, CHUNK], at=two)
            prod0 = sb("prod0", [P, 2, CHUNK], at=two)
            wgu_hi = sb("wgu_hi", [P, KD, UNITS * 2 * P], F32R, at=two)
            wgu_lo = sb("wgu_lo", [P, KD, UNITS * 2 * P], F32R, at=two)
            wd_hi = sb("wd_hi", [P, UNITS, D], F32R, at=two)
            wd_lo = sb("wd_lo", [P, UNITS, D], F32R, at=two)
            wr_hi = sb("wr_hi", [P, KD, R0], F32R, at=two)
            wr_lo = sb("wr_lo", [P, KD, R0], F32R, at=two)
            x_hi = sb("x_hi", [P, 2, KD, CHUNK], F32R, at=two)
            x_lo = sb("x_lo", [P, 2, KD, CHUNK], F32R, at=two)
            act_hi = sb("act_hi", [P, 2, CHUNK], F32R, at=two)
            act_lo = sb("act_lo", [P, 2, CHUNK], F32R, at=two)
            w_hi_ready, w_lo_ready, wd_lo_ready, x_hi_ready = (sem("w_hi_ready"), sem("w_lo_ready"), sem("wd_lo_ready"),
                                                               sem("x_hi_ready"))
            lg = sb("logits", [P, 2, CT, R0], at=two)
            v8 = sb("top8", [P, 2, CT, 8], at=two)
            taken = sb("taken", [P, 2, CT, E0], at=two)
            z = sb("z", [P, 2, 2, CT], at=two)
            th = sb("th", [P, 2, 2, CT], at=two)
            wlow = sb("wlow", [P, 2, CT], at=two)
            pick = sb("pick", [P, 2, CT, E0], at=two)
            cw = sb("cw", [P, 2, CT, E0 + 1], at=two)
            zrow = sb("zrow", [P, ROW], at=two)
            mask_u = sb("mask_u", [1, B * S], io["mask"].dtype, at=two)
            mask_in, mask_done, z_zero, z_done, cleared = (sem("mask_in"), sem("mask_done"), sem("z_zero"), sem("z_done"),
                                                           sem("cleared"))
            mt_ones, mt_in = sem("mt_ones"), [sem("mt_in0"), sem("mt_in1")]
            ap_mm, ap_out, lg_mm, lg_out = sem("ap_mm"), sem("ap_out"), sem("lg_mm"), sem("lg_out")
            z_ready, th_ready, cw_ready = sem("z_ready"), sem("th_ready"), sem("cw_ready")
            CR = 2
            gate_mm, up_mm, sg_ready, prod_ready, hi_ready, lo_ready, down_mm, unit_added = (
                sem("gate_mm"), sem("up_mm"), sem("sg_ready"), sem("prod_ready"), sem("hi_ready"), sem("lo_ready"),
                sem("down_mm"), sem("unit_added"))
            d2 = sem("dve_steps_2")
            QB = CHUNKS

            def chunks_pipelined(eng, prepare, main, chain=None, per=0):
                prepare(0, 0)
                with eng.Fori(0, CHUNKS // 2 - 1) as i:
                    if chain:
                        chain.enter(i, per)
                    main(2 * i, 0, 2 * i + 1)
                    main(2 * i + 1, 1, 2 * i + 2)
                if chain:
                    chain.leave(CHUNKS // 2 - 1)
                main(CHUNKS - 2, 0, CHUNKS - 1)
                main(CHUNKS - 1, 1, None)

            with nc.Block() as block:
                @block.sync
                def _(sp):
                    sp.dma_start(mask_u[:], io["mask"].rearrange("b s -> (b s)").rearrange("(a n) -> a n", a=1))\
                      .then_inc(mask_in, 16)
                    sp.wait_ge(mt_ones, 1)
                    for c in range(2):
                        sp.dma_start(mt[0:S, c, :], bass.AP(w_d.tensor, c * CHUNK, [[1, S], [1, CHUNK]])).then_inc(mt_in[c], 16)

                    RS, RY = SLOTS // P // CHUNKS, T * K1 // P // CHUNKS
                    slots_v = slots_d.rearrange("(p c r) w -> p c r w", p=P, c=CHUNKS)
                    y_v = y_d.rearrange("(p c r) w -> p c r w", p=P, c=CHUNKS)

                    def clear(c):
                        sp.dma_start(slots_v[:, bass.ds(c, 1), :, :].rearrange("p a r w -> p (a r) w"),
                                     bass.AP(zrow[:].tensor, 0, [[ROW, P], [0, RS], [1, ROW]])).then_inc(cleared, 16)
                        sp.dma_start(y_v[:, bass.ds(c, 1), :, :].rearrange("p a r w -> p (a r) w"),
                                     bass.AP(zrow[:].tensor, 0, [[ROW, P], [0, RY], [1, D]])).then_inc(cleared, 16)

                    sp.wait_ge(z_done, 1)
                    clear(0)
                    clear(1)
                    with sp.Fori(0, CHUNKS // 2 - 1) as i:
                        for par in range(2):
                            sp.wait_ge(ap_mm, 2 * i + (par + 1))
                            rows = bass.AP(w_d.tensor, par * CHUNK, [[WROW, B], [1, S], [1, CHUNK]])
                            sp.dma_start(mt[0:S, par, :], rows[bass.ds(i + 1, 1), :, :]).then_inc(mt_in[par], 16)
                            clear(2 * i + (par + 2))
                    for par in range(2):
                        sp.wait_ge(mt_in[par], 16 * (CHUNKS // 2))
                    sp.wait_ge(cleared, 32 * CHUNKS)

                @block.gpsimd
                def _(pool):
                    pool.sem_inc(lo_ready, CR)
                    pool.memset(zrow[:], 0.0).then_inc(z_zero, 1)
                    pool.memset(onerow[:], 1.0).then_inc(mask_done, 1)
                    pool.wait_ge(z_zero, 1)
                    pool.memset(zrow[:, D:D + 1].bitcast(I32), int(FAR)).then_inc(z_done, 1)
                    pool.wait_ge(mask_in, 16)
                    pool.tensor_scalar(mrow[:].rearrange("p b s -> p (b s)"), mask_u[:], MASKED, None, ALU.mult)\
                        .then_inc(mask_done, 1)

                    def low_part(c, u):
                        g = UNITS * c + u
                        pool.wait_ge(hi_ready, g + (CR + 1))
                        pool.wait_ge(down_mm, g + (CR - 1))
                        pool.tensor_tensor(act_lo[:, u % 2, :], prod0[:, u % 2, :], act_hi[:, u % 2, :].bitcast(F32),
                                           ALU.subtract).then_inc(lo_ready, 1)

                    def prepare(c, par):
                        ln_rstd_job(pool, c + QB, par)
                        pool.wait_ge(w_hi_ready, 2 * UNITS + 1)
                        pool.tensor_tensor(wd_lo[:], wd0[:], wd_hi[:].bitcast(F32), ALU.subtract).then_inc(wd_lo_ready, 1)
                        low_part(c, 0)
                        low_part(c, 1)

                    def main(c, par, nxt):
                        for u in range(2, UNITS):
                            low_part(c, u)
                            if nxt is not None and u == 3:
                                ln_rstd_job(pool, nxt + QB, 1 - par)
                        if nxt is not None:
                            low_part(nxt, 0)
                            low_part(nxt, 1)

                    chunks_pipelined(pool, prepare, main)

                @block.scalar
                def _(act):
                    act.sem_inc(sg_ready, CR)
                    act.sem_inc(hi_ready, CR)
                    act.activation(wr_hi[:], wr0[:], ACT.Copy).then_inc(w_hi_ready, 1)
                    for u in range(UNITS):
                        cols = slice(2 * u * P, 2 * (u + 1) * P)
                        act.activation(wgu_hi[:, :, cols], wgu0[:, :, cols], ACT.Copy).then_inc(w_hi_ready, 1)
                    for u in range(UNITS):
                        act.activation(wd_hi[:, u, :], wd0[:, u, :], ACT.Copy).then_inc(w_hi_ready, 1)

                    def evict(c, par):
                        act.wait_ge(ln_T, c + (QB + 1))
                        want(act, up_mm, UNITS * c - (UNITS - CR))
                        for k in range(KD):
                            act.activation(x_hi[:, par, k, :], bank[:, k, :], ACT.Copy).then_inc(x_hi_ready, 1)

                    def tanh(c, par):
                        act.wait_ge(z_ready, c + 1)
                        want(act, cw_ready, c - 1)
                        act.activation(th[:, par, :, :], z[:, par, :, :], ACT.Tanh, scale=0.5).then_inc(th_ready, 1)

                    def unit(c, u):
                        g = UNITS * c + u
                        act.wait_ge(gate_mm, g + (CR + 1))
                        act.wait_ge(prod_ready, g + (CR - 1))
                        act.activation(sg[:, u % 2, :], bank[:, 4 + u % 2, :], ACT.Silu).then_inc(sg_ready, 1)
                        act.wait_ge(prod_ready, g + (CR + 1))
                        act.wait_ge(down_mm, g + (CR - 1))
                        act.activation(act_hi[:, u % 2, :], prod0[:, u % 2, :], ACT.Copy).then_inc(hi_ready, 1)

                    def prepare(c, par):
                        evict(c, par)
                        tanh(c, par)
                        unit(c, 0)
                        unit(c, 1)

                    def main(c, par, nxt):
                        for u in range(2, UNITS):
                            unit(c, u)
                            if nxt is not None and u == 5:
                                evict(nxt, 1 - par)
                            if nxt is not None and u == 10:
                                tanh(nxt, 1 - par)
                        if nxt is not None:
                            unit(nxt, 0)
                            unit(nxt, 1)

                    chunks_pipelined(act, prepare, main)

                @block.vector
                def _(dve):
                    step = Chain(dve, d2, passed)
                    dve.sem_inc(prod_ready, CR)
                    dve.sem_inc(unit_added, CR)
                    dve.memset(mt[64:S + 1, :, :], 1.0).then_inc(mt_ones, 1)
                    dve.wait_ge(w_hi_ready, 1)
                    dve.tensor_tensor(wr_lo[:], wr0[:], wr_hi[:].bitcast(F32), ALU.subtract).then_inc(w_lo_ready, 1)
                    for u in range(UNITS):
                        dve.wait_ge(w_hi_ready, u + 2)
                        cols = slice(2 * u * P, 2 * (u + 1) * P)
                        dve.tensor_tensor(wgu_lo[:, :, cols], wgu0[:, :, cols], wgu_hi[:, :, cols].bitcast(F32),
                                          ALU.subtract).then_inc(w_lo_ready, 1)

                    def add_attention(c, par):
                        dve.wait_ge(ap_mm, c + 1)
                        dve.tensor_tensor(x[:, bass.ds(c * CT, CT), :], x[:, bass.ds(c * CT, CT), :],
                                          bank[:, 0:2, :].rearrange("p a (t n) -> p (a t) n", n=D), ALU.add).then_inc(ap_out, 1)
                        dve.wait_ge(ap_out, c + 1)
                        ln_stats_job(dve, c + QB, c, par)

                    def route(c, par):
                        dve.wait_ge(lg_mm, c + 1)
                        dve.tensor_copy(lg[:, par, :, :], bank[:, 0, 0:CT * R0].rearrange("p (t e) -> p t e", e=R0))\
                           .then_inc(lg_out, 1)
                        wait_apart(dve, lg_out, c + 1, passed)
                        for t in range(CT):
                            last = dve.max(v8[:, par, t, :], lg[:, par, t, 0:E0])
                        step(last)
                        dve.tensor_tensor(z[:, par, 0, :], v8[:, par, :, 0], v8[:, par, :, 1], ALU.subtract)
                        dve.tensor_copy(z[:, par, 1, :], lg[:, par, :, E0]).then_inc(z_ready, 1)
                        step(dve.memset(v8[:, par, :, 2:8], SENTINEL))
                        for t in range(CT):
                            last = dve.match_replace(taken[:, par, t, :], v8[:, par, t, :], lg[:, par, t, 0:E0], NEG)
                        step(last)

                    def weigh(c, par):
                        def over(ap):
                            return ap.rearrange("p (t a) -> p t a", a=1).broadcast_to([P, CT, E0])
                        dve.wait_ge(th_ready, c + 1)
                        step(dve.tensor_scalar(wlow[:, par, :], th[:, par, 0, :], -0.5, 0.5, ALU.mult, ALU.add))
                        step(dve.tensor_tensor(pick[:, par, :, :], lg[:, par, :, 0:E0], over(v8[:, par, :, 0]), ALU.is_equal))
                        step(dve.tensor_tensor(pick[:, par, :, :], pick[:, par, :, :], over(th[:, par, 0, :]), ALU.mult))
                        step(dve.tensor_tensor(pick[:, par, :, :], pick[:, par, :, :], over(wlow[:, par, :]), ALU.add))
                        dve.scalar_tensor_tensor(cw[:, par, :, 0:E0], taken[:, par, :, :], NEG, pick[:, par, :, :],
                                                 ALU.is_equal, ALU.mult)
                        step(dve.tensor_scalar(cw[:, par, :, E0], th[:, par, 1, :], 0.5, 0.5, ALU.mult, ALU.add))
                        dve.tensor_scalar(cw[:, par, :, :], cw[:, par, :, :], tg[:, 2:3], None, ALU.mult).then_inc(cw_ready, 1)

                    def low_parts(c, par):
                        dve.wait_ge(x_hi_ready, 2 * c + 2)
                        want(dve, up_mm, UNITS * c - (UNITS - CR))
                        for k in range(KD):
                            dve.tensor_tensor(x_lo[:, par, k, :], bank[:, k, :], x_hi[:, par, k, :].bitcast(F32),
                                              ALU.subtract).then_inc(ln_xT, 1)

                    def product(c, u):
                        g = UNITS * c + u
                        dve.wait_ge(up_mm, g + (CR + 1))
                        dve.wait_ge(sg_ready, g + (CR + 1))
                        dve.wait_ge(lo_ready, g + (CR - 1))
                        dve.tensor_tensor(prod0[:, u % 2, :], bank[:, 6 + u % 2, :], sg[:, u % 2, :], ALU.mult)\
                           .then_inc(prod_ready, 1)

                    def add_unit(c, par, u):
                        g = UNITS * c + u
                        if u == 0:
                            dve.wait_ge(cw_ready, c + 1)
                        dve.wait_ge(down_mm, g + (CR + 1))
                        dve.wait_ge(unit_added, g + CR)
                        for t in range(CT):
                            row = x[:, bass.ds(c * CT + t, 1), :].rearrange("p a n -> p (a n)")
                            last = dve.scalar_tensor_tensor(row, bank[:, 2 + t // 2, (t % 2) * D:(t % 2 + 1) * D],
                                                            cw[:, par, t, min(u, E0):min(u, E0) + 1], row,
                                                            ALU.mult, ALU.add)
                        last.then_inc(unit_added, 1)

                    def prepare(c, par):
                        add_attention(c, par)
                        ln_norm_job(dve, c + QB, c, par)
                        low_parts(c, par)
                        route(c, par)
                        weigh(c, par)
                        product(c, 0)
                        product(c, 1)

                    def main(c, par, nxt):
                        for u in range(2, UNITS + 2):
                            if u < UNITS:
                                product(c, u)
                            elif nxt is not None:
                                product(nxt, u - UNITS)
                            add_unit(c, par, u - 2)
                            if nxt is not None:
                                if u == 2:
                                    add_attention(nxt, 1 - par)
                                if u == 4:
                                    ln_norm_job(dve, nxt + QB, nxt, 1 - par)
                                if u == 6:
                                    low_parts(nxt, 1 - par)
                                if u == 9:
                                    route(nxt, 1 - par)
                                if u == 11:
                                    weigh(nxt, 1 - par)

                    chunks_pipelined(dve, prepare, main, step, 16)

                @block.tensor
                def _(pe):
                    pe.sem_inc(gate_mm, CR)
                    pe.sem_inc(up_mm, CR)
                    pe.sem_inc(down_mm, CR)

                    def product3(to, a_hi, a_lo, b_hi, b_lo, start, stop):
                        pe.matmul(to, a_hi, b_hi, start=start, stop=False)
                        pe.matmul(to, a_hi, b_lo, start=False, stop=False)
                        return pe.matmul(to, a_lo, b_hi, start=False, stop=stop)

                    def attention(c, par):
                        pe.wait_ge(mt_in[par], 16 * (c // 2) + 16)
                        want(pe, lg_out, c)
                        for t in range(CT):
                            last = pe.matmul(bank[:, t // 2, (t % 2) * D:(t % 2 + 1) * D], mt[:, par, t * P:(t + 1) * P],
                                             vwo0[:, bass.ds(c // 2, 1), :].rearrange("p a n -> p (a n)"),
                                             start=True, stop=True)
                        last.then_inc(ap_mm, 1)

                    def logits(c, par):
                        pe.wait_ge(ln_xT, 2 * c + (2 * QB + 2))
                        for t in range(CT):
                            for k in range(KD):
                                tok = slice(t * P, (t + 1) * P)
                                last = product3(bank[:, 0, t * R0:(t + 1) * R0], x_hi[:, par, k, tok], x_lo[:, par, k, tok],
                                                wr_hi[:, k, :], wr_lo[:, k, :], k == 0, k == KD - 1)
                        last.then_inc(lg_mm, 1)

                    def gate_up(c, par, u):
                        g = UNITS * c + u
                        for half, free, done, to in ((0, sg_ready, gate_mm, 4), (1, prod_ready, up_mm, 6)):
                            pe.wait_ge(free, g + (CR - 1))
                            cols = slice((2 * u + half) * P, (2 * u + half + 1) * P)
                            for k in range(KD):
                                last = product3(bank[:, to + u % 2, :], wgu_hi[:, k, cols], wgu_lo[:, k, cols],
                                                x_hi[:, par, k, :], x_lo[:, par, k, :], k == 0, k == KD - 1)
                            last.then_inc(done, 1)

                    def down(c, u):
                        g = UNITS * c + u
                        pe.wait_ge(lo_ready, g + (CR + 1))
                        pe.wait_ge(unit_added, g + CR)
                        for t in range(CT):
                            tok = slice(t * P, (t + 1) * P)
                            last = product3(bank[:, 2 + t // 2, (t % 2) * D:(t % 2 + 1) * D], act_hi[:, u % 2, tok],
                                            act_lo[:, u % 2, tok], wd_hi[:, u, :], wd_lo[:, u, :], True, True)
                        last.then_inc(down_mm, 1)

                    def prepare(c, par):
                        attention(c, par)
                        ln_transpose_job(pe, c + QB, par)
                        pe.wait_ge(w_lo_ready, UNITS + 1)
                        logits(c, par)
                        gate_up(c, par, 0)
                        gate_up(c, par, 1)
                        pe.wait_ge(wd_lo_ready, 1)

                    def main(c, par, nxt):
                        for u in range(2, UNITS + 2):
                            if u < UNITS:
                                gate_up(c, par, u)
                            elif nxt is not None:
                                gate_up(nxt, 1 - par, u - UNITS)
                            down(c, u - 2)
                            if nxt is not None:
                                if u == 2:
                                    attention(nxt, 1 - par)
                                if u == 5:
                                    ln_transpose_job(pe, nxt + QB, 1 - par)
                                if u == 8:
                                    logits(nxt, 1 - par)

                    chunks_pipelined(pe, prepare, main)
        early.close()


        three = ExitStack()
        with three:
            JC = -(-HS // P)
            JL = HS - (JC - 1) * P
            SPLIT = [(0, 6), (6, 6), (12, 4)]
            wqk = sb("wqk", [P, 2, KD, HS], at=three)
            wqk_hi = sb("wqk_hi", [P, 2, KD, HS], F32R, at=three)
            wqk_lo = sb("wqk_lo", [P, 2, KD, HS], F32R, at=three)
            vwo = sb("vwo", [P, 2, JC * D], at=three)
            vwo_hi = sb("vwo_hi", [P, 2, JC * D], F32R, at=three)
            vwo_lo = sb("vwo_lo", [P, 2, JC * D], F32R, at=three)
            QS, VS = HS // 8, JC * D // 8
            sgu = sb("shared_gate_up", [P, KD, 2 * P], at=three)
            sdn = sb("shared_down", [P, D], at=three)
            wr1 = sb("wr1", [P, KD, E1], at=three)
            tri = sb("tri", [P, P], BF16, at=three)
            allone = sb("allone", [P, P], BF16, at=three)
            ebase = sb("ebase", [P, E1], at=three)
            kth = sb("kth", [P, K1, E1], at=three)
            onesf = sb("onesf", [P, E1], at=three)
            outrow = sb("outrow", [P, TILES, K1], I32, at=three)
            ln = {}
            for s in "ab":
                ln[s] = dict(bst=sb(f"bst_{s}", [P, 2, 6], at=three), mv=sb(f"mv_{s}", [P, 2, 2], at=three),
                             veps=sb(f"veps_{s}", [P, 2, 1], at=three), rstd=sb(f"rstd_{s}", [P, 2, 1], at=three),
                             summed=sem(f"{s}_summed"), stats=sem(f"{s}_stats"), eps=sem(f"{s}_eps"),
                             ready=sem(f"{s}_rstd_ready"))
            xa = sb("xa", [P, 2, D], at=three)
            xa_hi = sb("xa_hi", [P, 2, KD * P], F32R, at=three)
            xa_lo = sb("xa_lo", [P, 2, KD * P], F32R, at=three)
            rows = sb("rows", [P, 2, K1, ROW], at=three)
            xbT = sb("xbT", [P, 2, KD, P], at=three)
            att = sb("att", [P, 2, HS], at=three)
            attT_hi = sb("attT_hi", [P, JC * P], F32R, at=three)
            attT_lo = sb("attT_lo", [P, JC * P], F32R, at=three)
            mx = sb("mx", [P, 2, 2, H1], at=three)
            den = sb("den", [P, 2, 2, H1], at=three)
            lg1 = sb("lg1", [P, 2, E1], at=three)
            t8 = sb("t8", [P, 2, 8], at=three)
            ngm = sb("ngm", [P, 2, 1], at=three)
            tk = sb("tk", [P, 2, E1], at=three)
            ew = sb("ew", [P, 2, E1], at=three)
            msel = sb("msel", [P, 2, E1], at=three)
            mselb = sb("mselb", [P, 2, E1], BF16, at=three)
            cum = sb("cum", [P, 2, E1], BF16, at=three)
            ws1 = sb("ws1", [P, 2, 2], at=three)
            wn = sb("wn", [P, 2, E1], at=three)
            key = sb("key", [P, 2, E1], at=three)
            hot = sb("hot", [P, 2, K1, E1], at=three)
            prod = sb("prod", [P, 2, K1, E1], at=three)
            far = sb("far", [P, 2, E1], at=three)
            slot = sb("slot", [P, 2, E1], at=three)
            slotk = sb("slotk", [P, 2, K1], at=three)
            place = sb("place", [P, 2, K1], I32, at=three)
            thg = sb("thg", [P, 2, P], at=three)
            hid = sb("hid", [P, 2, P], at=three)
            actS = sb("actS", [P, 2, P], at=three)

            w3_in, wqk_in, vwo_in = sem("w3_in"), sem("wqk_in"), sem("vwo_in")
            wqk_hi_ready, wqk_lo_ready, vwo_hi_ready, vwo_lo_ready = (sem("wqk_hi_ready"), sem("wqk_lo_ready"),
                                                                      sem("vwo_hi_ready"), sem("vwo_lo_ready"))
            a_hi, at_hi, vwo_zero = sem("a_hi"), sem("at_hi"), sem("vwo_zero")
            HP, last_ready = SPLIT[2][0], sem("last_ready")
            c3, c3_zero = sem("consts3"), sem("consts3_zero")
            a_xn, a_T, a_xT = sem("a_xn"), sem("a_T"), sem("a_xT")
            e_mm, mx_ready, exp_done, den_ready, att_ready = (sem("e_mm"), sem("mx_ready"), sem("exp_done"),
                                                              sem("den_ready"), sem("att_ready"))
            at_T, at_out, av_mm, av_added = sem("at_T"), sem("at_out"), sem("av_mm"), sem("av_added")
            b_xn, b_T, b_xT = sem("b_xn"), sem("b_T"), sem("b_xT")
            r_mm, r_out, ngm_ready, ew_ready, msel_ready = (sem("r_mm"), sem("r_out"), sem("ngm_ready"),
                                                            sem("ew_ready"), sem("msel_ready"))
            thg_ready, actS_ready, sd_mm, sd_added = (sem("thg_ready"), sem("actS_ready"),
                                                             sem("sd_mm"), sem("sd_added"))
            pos_mm, pos_read, place_ready = sem("pos_mm"), sem("pos_read"), sem("place_ready")
            sent = [sem("sent0"), sem("sent1")]
            d3 = sem("dve_steps_3")

            def steps_pipelined(eng, first, step_fn, chain=None, per=0):
                first()
                def run(n, par):
                    step_fn(n, par, n < TILES, 1 <= n <= TILES, 2 <= n < TILES + 2, 3 <= n)
                for n in range(4):
                    run(n, n % 2)
                rounds = (TILES - 6) // 2
                with eng.Fori(0, rounds) as i:
                    if chain:
                        chain.enter(i, per)
                    for par in range(2):
                        step_fn(2 * i + (4 + par), par, True, True, True, True)
                if chain:
                    chain.leave(rounds)
                for n in range(TILES - 2, TILES + 3):
                    run(n, n % 2)

            def wqk_slice(n):
                return lambda w: w[:, bass.ds((n // 8 + 1) % 2, 1), :, bass.ds(n % 8 * QS, QS)].rearrange("p a k n -> p (a k) n")

            def vwo_slice(n):
                return lambda w: w[:, bass.ds((n // 8 + 1) % 2, 1), bass.ds(n % 8 * VS, VS)].rearrange("p a n -> p (a n)")

            def scale_heads(eng, par, h0, h1):
                heads = att[:, par, h0 * S:h1 * S].rearrange("p (h s) -> p h s", s=S)
                over = den[:, par, 1, h0:h1].rearrange("p (h a) -> p h a", a=1).broadcast_to([P, h1 - h0, S])
                return eng.tensor_tensor(heads, heads, over, ALU.mult)

            def tile(n):
                return x[:, bass.ds(n, 1), :].rearrange("p a n -> p (a n)")

            def ln_stats_tile(dve, s, n, par):
                r = ln[s]
                dve.bn_stats(r["bst"][:, par, :], tile(n)).then_inc(r["summed"], 1)
                wait_apart(dve, r["summed"], n + 1, passed)
                dve.bn_aggr(r["mv"][:, par, :], r["bst"][:, par, :]).then_inc(r["stats"], 1)

            def ln_rstd_tile(pool, s, n, par):
                r = ln[s]
                wait_apart(pool, r["stats"], n + 1, passed_pool)
                pool.tensor_scalar_add(r["veps"][:, par, :], r["mv"][:, par, 1:2], EPS).then_inc(r["eps"], 1)
                pool.wait_ge(r["eps"], n + 1)
                pool.tensor_tensor(r["rstd"][:, par, :], r["veps"][:, par, :], neghalf[:, 0:1], ALU.pow)\
                    .then_inc(r["ready"], 1)

            with nc.Block() as block:
                @block.sync
                def _(sp):
                    sp.dma_start(sgu[:], io["sgu1"].rearrange("(k p) n -> p k n", p=P)).then_inc(w3_in, 16)
                    sp.dma_start(sdn[:], io["sd1"]).then_inc(w3_in, 16)
                    sp.dma_start(wr1[:], io["wr1"].rearrange("(k p) n -> p k n", p=P)).then_inc(w3_in, 16)
                    sp.wait_ge(vwo_zero, 2)
                    for b in range(B):
                        if b >= 2:
                            sp.wait_ge(wqk_lo_ready, 8 * (b - 2) + 1)
                        sp.dma_start(wqk[:, b % 2, :, :], wqk_d[b].rearrange("(k p) n -> p k n", p=P)).then_inc(wqk_in, 16)
                        sp.wait_ge(wqk_in, 16 * (b + 1))
                        if b >= 2:
                            sp.wait_ge(vwo_lo_ready, 8 * (b - 2) + 1)
                        sp.dma_start(vwo[:, b % 2, 0:(JC - 1) * D].rearrange("p (j n) -> p j n", n=D),
                                     vwo_d[b, 0:(JC - 1) * P, :].rearrange("(j p) n -> p j n", p=P)).then_inc(vwo_in, 16)
                        sp.dma_start(vwo[0:JL, b % 2, (JC - 1) * D:], vwo_d[b, (JC - 1) * P:HS, :]).then_inc(vwo_in, 16)
                        sp.wait_ge(vwo_in, 32 * (b + 1))
                    sp.sem_inc(wqk_in, 16)
                    sp.sem_inc(vwo_in, 32)
                    sp.wait_ge(w3_in, 48)

                @block.gpsimd
                def _(pool):
                    def first():
                        pool.memset(tri[:], 1.0).then_inc(c3_zero, 1)
                        pool.memset(allone[:], 1.0).then_inc(c3, 1)
                        pool.memset(onesf[:], 1.0).then_inc(c3, 1)
                        pool.memset(cum[:, 0, :], 0.0).then_inc(c3, 1)
                        pool.memset(rows[:], 0.0).then_inc(c3, 1)
                        for k in range(K1):
                            pool.memset(kth[:, k, :], 1.0 + k).then_inc(c3, 1)
                        pool.iota(outrow[:], pattern=[[K1 * P, TILES], [1, K1]], base=0, channel_multiplier=K1).then_inc(c3, 1)
                        pool.iota(ebase[:], pattern=[[CAP, E1]], base=0, channel_multiplier=0,
                                  allow_small_or_imprecise_dtypes=True).then_inc(c3, 1)
                        pool.wait_ge(c3_zero, 1)
                        pool.affine_select(out=tri[:], in_=tri[:], compare_op=ALU.is_gt, fill=0.0, base=0,
                                           pattern=[[1, P]], channel_multiplier=-1).then_inc(c3, 1)
                        ln_rstd_tile(pool, "a", 0, 0)
                        pool.wait_ge(wqk_hi_ready, 1)
                        pool.tensor_tensor(wqk_lo[:, 0, :, :], wqk[:, 0, :, :], wqk_hi[:, 0, :, :].bitcast(F32), ALU.subtract)\
                            .then_inc(wqk_lo_ready, 1)
                        pool.wait_ge(vwo_hi_ready, 1)
                        pool.tensor_tensor(vwo_lo[:, 0, :], vwo[:, 0, :], vwo_hi[:, 0, :].bitcast(F32), ALU.subtract)\
                            .then_inc(vwo_lo_ready, 1)

                    def step(n, par, scores, values, route, dispatch):
                        if route:
                            ln_rstd_tile(pool, "b", n - 2, par)
                        if scores and (not isinstance(n, int) or n + 1 < TILES):
                            ln_rstd_tile(pool, "a", n + 1, 1 - par)
                        if scores and (not isinstance(n, int) or n + 2 < TILES):
                            pool.wait_ge(wqk_hi_ready, n + 2)
                            q = wqk_slice(n)
                            pool.tensor_tensor(q(wqk_lo), q(wqk), q(wqk_hi).bitcast(F32), ALU.subtract)\
                                .then_inc(wqk_lo_ready, 1)
                            if not isinstance(n, int) or n:
                                pool.wait_ge(vwo_hi_ready, n + 1)
                                v = vwo_slice(n - 1)
                                pool.tensor_tensor(v(vwo_lo), v(vwo), v(vwo_hi).bitcast(F32), ALU.subtract)\
                                    .then_inc(vwo_lo_ready, 1)
                        if dispatch:
                            wait_apart(pool, place_ready, n - 2, passed_pool)
                            for k in range(K1):
                                pool.indirect_dma_start(
                                    slots_d, bass.IndirectOffsetOnAxis(ap=place[:, 1 - par, k:k + 1], axis=0),
                                    rows[:, 1 - par, k, :], None, bounds_check=SLOTS - 1, oob_is_err=False)\
                                    .then_inc(sent[1 - par], 16)
                        if scores:
                            pool.wait_ge(den_ready, n + 1)
                            scale_heads(pool, par, 0, HP).then_inc(att_ready, 1)

                    steps_pipelined(pool, first, step)
                    for par in range(2):
                        pool.wait_ge(sent[par], 16 * K1 * TILES // 2)

                @block.scalar
                def _(act):
                    def evict_a(n, par):
                        act.wait_ge(a_T, n + 1)
                        want(act, e_mm, n - 1)
                        act.activation(xa_hi[:, par, :], bank[:, 6, D:2 * D], ACT.Copy).then_inc(a_hi, 1)

                    def first():
                        evict_a(0, 0)
                        act.wait_ge(wqk_in, 16)
                        act.activation(wqk_hi[:, 0, :, :], wqk[:, 0, :, :], ACT.Copy).then_inc(wqk_hi_ready, 1)
                        act.wait_ge(vwo_in, 32)
                        act.activation(vwo_hi[:, 0, :], vwo[:, 0, :], ACT.Copy).then_inc(vwo_hi_ready, 1)

                    def evict_att(n, g):
                        act.wait_ge(at_T, 3 * n + (g + 1))
                        want(act, av_mm, n)
                        if g < 2:
                            act.activation(attT_hi[:, 4 * g * P:4 * (g + 1) * P], bank[:, 3 + g, :], ACT.Copy).then_inc(at_hi, 1)
                        else:
                            act.activation(attT_hi[:, 8 * P:9 * P], bank[:, 3, 0:P], ACT.Copy)
                            act.activation(attT_hi[0:JL, 9 * P:10 * P], bank[0:JL, 3, P:2 * P], ACT.Copy).then_inc(at_hi, 1)

                    def exps(n, par, a):
                        h0, count = SPLIT[a]
                        if a == 0:
                            act.wait_ge(mx_ready, n + 1)
                            want(act, att_ready, n - 1)
                            want(act, last_ready, n - 1)
                        for i in range(count):
                            h = h0 + i
                            last = act.activation(att[:, par, h * S:(h + 1) * S], bank[:, a, i * S:(i + 1) * S], ACT.Exp,
                                                  bias=mx[:, par, 1, h:h + 1], accum_out=den[:, par, 0, h:h + 1])
                        last.then_inc(exp_done, 1)

                    def step(n, par, scores, values, route, dispatch):
                        if scores and (not isinstance(n, int) or n + 2 < TILES):
                            act.wait_ge(wqk_in, 16 * (n // 8) + 32)
                            want(act, e_mm, n)
                            q = wqk_slice(n)
                            act.activation(q(wqk_hi), q(wqk), ACT.Copy).then_inc(wqk_hi_ready, 1)
                            if not isinstance(n, int) or n:
                                act.wait_ge(vwo_in, 32 * ((n - 1) // 8) + 64)
                                want(act, av_mm, n - 1)
                                v = vwo_slice(n - 1)
                                act.activation(v(vwo_hi), v(vwo), ACT.Copy).then_inc(vwo_hi_ready, 1)
                        if route:
                            act.wait_ge(b_T, n - 1)
                            want(act, r_mm, n - 3)
                            act.activation(xbT[:, par, :, :].rearrange("p k t -> p (k t)"), bank[:, 6, 0:D], ACT.Copy)\
                               .then_inc(b_xT, 1)
                        if values:
                            for g in range(3):
                                evict_att(n - 1, g)
                        if scores:
                            if not isinstance(n, int) or n + 1 < TILES:
                                evict_a(n + 1, 1 - par)
                            exps(n, par, 0)
                        if route:
                            act.wait_ge(r_out, n - 1)
                            want(act, actS_ready, n - 3)
                            act.activation(thg[:, par, :], bank[:, 7, 0:P], ACT.Tanh, scale=0.5).then_inc(thg_ready, 1)
                            act.wait_ge(ngm_ready, n - 1)
                            act.activation(ew[:, par, :], lg1[:, par, :], ACT.Exp, bias=ngm[:, par, :]).then_inc(ew_ready, 1)
                        if scores:
                            exps(n, par, 1)
                            exps(n, par, 2)

                    steps_pipelined(act, first, step)

                @block.vector
                def _(dve):
                    chain = Chain(dve, d3, passed)

                    def norm_a(n, par):
                        dve.wait_ge(ln["a"]["ready"], n + 1)
                        want(dve, a_T, n - 1)
                        dve.tensor_scalar(xa[:, par, :], tile(n), ln["a"]["mv"][:, par, 0:1], ln["a"]["rstd"][:, par, :],
                                          ALU.subtract, ALU.mult).then_inc(a_xn, 1)

                    def largest(n, par):
                        dve.wait_ge(e_mm, n + 1)
                        want(dve, exp_done, 3 * n - 3)
                        for a, (h, count) in enumerate(SPLIT):
                            e = bank[:, a, 0:count * S].rearrange("p (h s) -> p h s", s=S)
                            last = dve.tensor_reduce(mx[:, par, 0, h:h + count], e, AX.X, ALU.max)
                        chain(last)
                        dve.tensor_scalar(mx[:, par, 1, :], mx[:, par, 0, :], -1.0, None, ALU.mult).then_inc(mx_ready, 1)

                    def low_a(n, par):
                        dve.wait_ge(a_hi, n + 1)
                        want(dve, e_mm, n - 1)
                        dve.tensor_tensor(xa_lo[:, par, :], bank[:, 6, D:2 * D], xa_hi[:, par, :].bitcast(F32), ALU.subtract)\
                           .then_inc(a_xT, 1)

                    def low_att(n, g):
                        dve.wait_ge(at_hi, 3 * n + (g + 1))
                        want(dve, av_mm, n)
                        for j, w, p1 in ((4 * g, 4, P),) if g < 2 else ((8, 1, P), (9, 1, JL)):
                            cols = slice(j * P, (j + w) * P)
                            at = (j - 4 * g) % 4 * P
                            last = dve.tensor_tensor(attT_lo[0:p1, cols], bank[0:p1, 3 + g % 2, at:at + w * P],
                                                     attT_hi[0:p1, cols].bitcast(F32), ALU.subtract)
                        last.then_inc(at_out, 1)

                    def denominators(n, par):
                        dve.wait_ge(exp_done, 3 * n + 2)
                        dve.reciprocal(den[:, par, 1, 0:HP], den[:, par, 0, 0:HP]).then_inc(den_ready, 1)

                    def last_heads(n, par):
                        dve.wait_ge(exp_done, 3 * n + 3)
                        return chain.mark(dve.reciprocal(den[:, par, 1, HP:H1], den[:, par, 0, HP:H1]))

                    def over_k(ap):
                        return ap.rearrange("p (a e) -> p a e", a=1).broadcast_to([P, K1, E1])

                    def norm_b(n, par):
                        dve.wait_ge(ln["b"]["ready"], n + 1)
                        want(dve, b_T, n - 1)
                        want(dve, sent[par], 64 * (n // 2))
                        src = tile(n).rearrange("p (a n) -> p a n", a=1).broadcast_to([P, K1, D])
                        dve.tensor_copy(rows[:, par, :, D:D + 1].bitcast(I32),
                                        outrow[:, bass.ds(n, 1), :].rearrange("p a k -> p k a"))
                        dve.tensor_scalar(rows[:, par, :, 0:D], src, ln["b"]["mv"][:, par, 0:1], ln["b"]["rstd"][:, par, :],
                                          ALU.subtract, ALU.mult).then_inc(b_xn, 1)

                    def first():
                        for b in range(2):
                            dve.memset(vwo[64:P, b, (JC - 1) * D:], 0.0).then_inc(vwo_zero, 1)
                        ln_stats_tile(dve, "a", 0, 0)
                        ln_stats_tile(dve, "a", 1, 1)
                        norm_a(0, 0)
                        dve.wait_ge(c3, 11)
                        low_a(0, 0)

                    def step(n, par, scores, values, routes, dispatch):
                        loop = not isinstance(n, int)
                        m, mp, r = n - 3, 1 - par, n - 2
                        ahead = scores and (loop or n + 1 < TILES)
                        stats = scores and (loop or n + 2 < TILES)
                        if dispatch:
                            dve.wait_ge(pos_mm, m + 1)
                            pos = bank[:, 7, 288:288 + E1]
                            dve.tensor_scalar(far[:, mp, :], pos, float(CAP), FAR, ALU.is_ge, ALU.mult)
                            slots = chain.mark(dve.tensor_tensor(slot[:, mp, :], pos, ebase[:], ALU.add))
                            chain.need(slots)
                            dve.tensor_tensor(slot[:, mp, :], slot[:, mp, :], far[:, mp, :], ALU.add).then_inc(pos_read, 1)
                        if routes:
                            norm_b(r, par)
                        if ahead:
                            norm_a(n + 1, 1 - par)
                        if scores:
                            largest(n, par)
                        if dispatch:
                            dve.wait_ge(sd_mm, m + 1)
                            dve.scalar_tensor_tensor(tile(m), bank[:, 5, D:2 * D], tg[:, 3:4], tile(m), ALU.mult, ALU.add)\
                               .then_inc(sd_added, 1)
                        if values:
                            low_att(n - 1, 0)
                        if dispatch:
                            dve.wait_ge(pos_read, m + 1)
                            picked = chain.mark(dve.tensor_tensor(prod[:, mp, :, :], hot[:, mp, :, :],
                                                                  over_k(slot[:, mp, :]), ALU.mult))
                        if values:
                            low_att(n - 1, 1)
                        if dispatch:
                            chain.need(picked)
                            picked = chain.mark(dve.tensor_reduce(slotk[:, mp, :], prod[:, mp, :, :], AX.X, ALU.add))
                        if routes:
                            dve.wait_ge(r_mm, r + 1)
                            dve.tensor_copy(lg1[:, par, :], bank[:, 7, 256:256 + E1]).then_inc(r_out, 1)
                        if dispatch:
                            chain.need(picked)
                            want(dve, sent[mp], 64 * (m // 2))
                            dve.tensor_copy(place[:, mp, :], slotk[:, mp, :]).then_inc(place_ready, 1)
                        if values:
                            low_att(n - 1, 2)
                        if routes:
                            wait_apart(dve, r_out, r + 1, passed)
                            top4 = chain.mark(dve.max(t8[:, par, :], lg1[:, par, :]))
                        if ahead:
                            low_a(n + 1, 1 - par)
                        if routes:
                            chain.need(top4)
                            dve.tensor_scalar(ngm[:, par, :], t8[:, par, 0:1], -1.0, None, ALU.mult).then_inc(ngm_ready, 1)
                            top4 = chain.mark(dve.memset(t8[:, par, K1:8], SENTINEL))
                        if stats:
                            wait_apart(dve, a_xn, n + 1, passed)
                            dve.bn_stats(ln["a"]["bst"][:, par, :], tile(n + 2)).then_inc(ln["a"]["summed"], 1)
                        if routes:
                            chain.need(top4)
                            took = chain.mark(dve.match_replace(tk[:, par, :], t8[:, par, :], lg1[:, par, :], NEG))
                        if stats:
                            wait_apart(dve, ln["a"]["summed"], n + 3, passed)
                            dve.bn_aggr(ln["a"]["mv"][:, par, :], ln["a"]["bst"][:, par, :]).then_inc(ln["a"]["stats"], 1)
                        if routes:
                            chain.need(took)
                            dve.tensor_scalar(mselb[:, par, :], tk[:, par, :], NEG, None, ALU.is_equal)
                            took = chain.mark(dve.tensor_scalar(msel[:, par, :], tk[:, par, :], NEG, None, ALU.is_equal))
                            dve.wait_ge(thg_ready, r + 1)
                            want(dve, sd_mm, r - 1)
                            half = chain.mark(dve.scalar_tensor_tensor(hid[:, par, :], thg[:, par, :], 1.0, bank[:, 7, 0:P],
                                                                       ALU.add, ALU.mult))
                            chain.need(took)
                            dve.tensor_tensor(cum[:, 1 - par, :], cum[:, par, :], mselb[:, par, :], ALU.add)\
                               .then_inc(msel_ready, 1)
                            rank = chain.mark(dve.tensor_tensor_scan(key[:, par, :], onesf[:], msel[:, par, :], 0.0,
                                                                     ALU.mult, ALU.add))
                            chain.need(half)
                            dve.scalar_tensor_tensor(actS[:, par, :], hid[:, par, :], 0.5, bank[:, 7, P:2 * P],
                                                     ALU.mult, ALU.mult).then_inc(actS_ready, 1)
                            chain.need(rank)
                            rank = chain.mark(dve.tensor_tensor(key[:, par, :], key[:, par, :], msel[:, par, :], ALU.mult))
                            dve.wait_ge(ew_ready, r + 1)
                            weight = chain.mark(dve.scalar_tensor_tensor(wn[:, par, :], msel[:, par, :], 1.0, ew[:, par, :],
                                                                         ALU.mult, ALU.mult, accum_out=ws1[:, par, 0:1]))
                            chain.need(rank)
                            rank = chain.mark(dve.tensor_tensor(hot[:, par, :, :], over_k(key[:, par, :]), kth[:], ALU.is_equal))
                            chain.need(weight)
                            weight = chain.mark(dve.reciprocal(ws1[:, par, 1:2], ws1[:, par, 0:1]))
                        if scores:
                            denominators(n, par)
                        if routes:
                            chain.need(weight)
                            weight = chain.mark(dve.tensor_scalar(wn[:, par, :], wn[:, par, :], ws1[:, par, 1:2], tg[:, 3:4],
                                                                  ALU.mult, ALU.mult))
                        if values:
                            dve.wait_ge(av_mm, n)
                            dve.tensor_tensor(tile(n - 1), tile(n - 1), bank[:, 5, 0:D], ALU.add).then_inc(av_added, 1)
                        if routes:
                            chain.need(weight)
                            weight = chain.mark(dve.tensor_tensor(prod[:, par, :, :], hot[:, par, :, :],
                                                                  over_k(wn[:, par, :]), ALU.mult))
                        if scores:
                            inverse = last_heads(n, par)
                        if values:
                            wait_apart(dve, av_added, n, passed)
                            wait_apart(dve, b_xn, n - 2, passed)
                            dve.bn_stats(ln["b"]["bst"][:, 1 - par, :], tile(n - 1)).then_inc(ln["b"]["summed"], 1)
                        if scores:
                            chain.need(inverse)
                            scale_heads(dve, par, HP, H1).then_inc(last_ready, 1)
                        if routes:
                            chain.need(weight)
                            weight = chain.mark(dve.tensor_reduce(wk[:, bass.ds(r, 1), :].rearrange("p a k -> p (a k)"),
                                                                  prod[:, par, :, :], AX.X, ALU.add))
                        if values:
                            wait_apart(dve, ln["b"]["summed"], n, passed)
                            dve.bn_aggr(ln["b"]["mv"][:, 1 - par, :], ln["b"]["bst"][:, 1 - par, :])\
                               .then_inc(ln["b"]["stats"], 1)
                        if routes:
                            chain.need(weight)

                    steps_pipelined(dve, first, step, chain, 36)

                @block.tensor
                def _(pe):
                    def product3(to, a_hi, a_lo, b_hi, b_lo, start, stop):
                        pe.matmul(to, a_hi, b_hi, start=start, stop=False)
                        pe.matmul(to, a_hi, b_lo, start=False, stop=False)
                        return pe.matmul(to, a_lo, b_hi, start=False, stop=stop)

                    def transpose_a(n, par):
                        pe.wait_ge(a_xn, n + 1)
                        want(pe, b_xT, n - 2)
                        want(pe, a_xT, n)
                        for k in range(KD):
                            last = pe.transpose(bank[:, 6, (KD + k) * P:(KD + k + 1) * P], xa[:, par, k * P:(k + 1) * P],
                                                ident[:])
                        last.then_inc(a_T, 1)

                    def first():
                        pe.wait_ge(w3_in, 48)
                        pe.wait_ge(c3, 11)
                        transpose_a(0, 0)

                    def score(n, par):
                        pe.wait_ge(wqk_lo_ready, 8 * (n // 8) + 1)
                        pe.wait_ge(a_xT, n + 1)
                        for a, (h, count) in enumerate(SPLIT):
                            wait_apart(pe, exp_done, 0 if isinstance(n, int) and n == 0 else 3 * n + (a - 2), passed_pe)
                            cols = slice(h * S, (h + count) * S)
                            to = bank[:, a, 0:count * S]
                            pe.matmul(to.rearrange("p (h s) -> p h s", s=S), onerow[0:1, :],
                                      mrow[0:1, bass.ds(n // 8, 1), :].broadcast_to([1, count, S]), start=True, stop=False)
                            for k in range(KD):
                                tok = slice(k * P, (k + 1) * P)
                                hi, lo = (w[:, bass.ds((n // 8) % 2, 1), k, cols].rearrange("p a n -> p (a n)")
                                          for w in (wqk_hi, wqk_lo))
                                last = product3(to, xa_hi[:, par, tok], xa_lo[:, par, tok], hi, lo, False, k == KD - 1)
                        last.then_inc(e_mm, 1)

                    def transpose_att(n, par, g):
                        if g == 0:
                            pe.wait_ge(att_ready, n + 1)
                        if g == 1:
                            pe.wait_ge(last_ready, n + 1)
                        want(pe, at_out, 3 * n + (g - 1 if g != 1 else -1))
                        for j in range(4 * g, min(4 * g + 4, JC)):
                            w = min(P, HS - j * P)
                            last = pe.transpose(bank[0:w, 3 + g % 2, (j % 4) * P:(j % 4 + 1) * P],
                                                att[:, par, j * P:j * P + w], ident[:])
                        last.then_inc(at_T, 1)

                    def values_mm(n, par):
                        pe.wait_ge(vwo_lo_ready, 8 * (n // 8) + 1)
                        want(pe, sd_added, n - 1)
                        want(pe, av_added, n)
                        for j in range(JC):
                            if j % 4 == 0:
                                wait_apart(pe, at_out, 3 * n + (j // 4 + 1), passed_pe)
                            w = min(P, HS - j * P)
                            hi, lo = (m[0:w, bass.ds((n // 8) % 2, 1), j * D:(j + 1) * D].rearrange("p a n -> p (a n)")
                                      for m in (vwo_hi, vwo_lo))
                            last = product3(bank[:, 5, 0:D], attT_hi[0:w, j * P:(j + 1) * P], attT_lo[0:w, j * P:(j + 1) * P],
                                            hi, lo, j == 0, j == JC - 1)
                        last.then_inc(av_mm, 1)

                    def step(n, par, scores, values, routes, dispatch):
                        loop = not isinstance(n, int)
                        if dispatch:
                            m, mp = n - 3, 1 - par
                            pe.wait_ge(msel_ready, m + 1)
                            pe.wait_ge(actS_ready, m + 1)
                            pe.matmul(bank[:, 7, 288:288 + E1], tri[:], mselb[:, mp, :], start=True, stop=False)
                            pe.matmul(bank[:, 7, 288:288 + E1], allone[:], cum[:, mp, :], start=False, stop=True)\
                              .then_inc(pos_mm, 1)
                        if scores:
                            score(n, par)
                        if dispatch:
                            pe.wait_ge(av_added, m + 2 if loop else min(m + 2, TILES))
                            pe.matmul(bank[:, 5, D:2 * D], actS[:, mp, :], sdn[:], start=True, stop=True).then_inc(sd_mm, 1)
                        if routes:
                            m = n - 2
                            pe.wait_ge(b_xn, m + 1)
                            pe.wait_ge(a_xT, n + 1 if loop else min(n + 1, TILES))
                            for k in range(KD):
                                last = pe.transpose(bank[:, 6, k * P:(k + 1) * P], rows[:, par, 0, k * P:(k + 1) * P], ident[:])
                            last.then_inc(b_T, 1)
                        if values:
                            transpose_att(n - 1, 1 - par, 0)
                            transpose_att(n - 1, 1 - par, 1)
                        if routes:
                            pe.wait_ge(b_xT, m + 1)
                            want(pe, pos_read, m)
                            for half in range(2):
                                for k in range(KD):
                                    last = pe.matmul(bank[:, 7, half * P:(half + 1) * P], sgu[:, k, half * P:(half + 1) * P],
                                                     xbT[:, par, k, :], start=k == 0, stop=k == KD - 1)
                            for k in range(KD):
                                last = pe.matmul(bank[:, 7, 256:256 + E1], xbT[:, par, k, :], wr1[:, k, :],
                                                 start=k == 0, stop=k == KD - 1)
                            last.then_inc(r_mm, 1)
                        if values:
                            transpose_att(n - 1, 1 - par, 2)
                        if scores and (loop or n + 1 < TILES):
                            transpose_a(n + 1, 1 - par)
                        if values:
                            values_mm(n - 1, 1 - par)

                    steps_pipelined(pe, first, step)

        four = ExitStack()
        with four:
            NB, NY = 8, 4
            BLK = CAP // P
            wgu = sb("expert_gate_up", [P, NB, KD, 2 * P], at=four)
            wd = sb("expert_down", [P, NB, D], at=four)
            xg = sb("expert_rows", [P, NB, BLK, ROW], at=four)
            target = sb("target_rows", [P, NY, BLK], I32, at=four)
            xgT = sb("expert_rowsT", [P, 2, KD, CAP], at=four)
            sgE = sb("expert_silu", [P, 2, CAP], at=four)
            hidT = sb("expert_hiddenT", [P, 2, CAP], at=four)
            y = sb("expert_out", [P, NY, BLK, D], at=four)
            in4 = x_in
            sent4 = [sem(f"expert_sent{i}") for i in range(NY)]
            g_T, g_xT, g_mm, g_silu, g_hid, g_down, g_y, targets = (
                sem("g_T"), sem("g_xT"), sem("g_mm"), sem("g_silu"), sem("g_hid"), sem("g_down"), sem("g_y"),
                sem("targets"))

            def experts_pipelined(eng, step_fn):
                def run(s):
                    step_fn(s, s % NB, s < E1, 1 <= s <= E1, s >= 2)
                for s in range(NB):
                    run(s)
                with eng.Fori(1, E1 // NB) as i:
                    for j in range(NB):
                        step_fn(NB * i + j, j, True, True, True)
                for s in range(E1, E1 + 2):
                    run(s)

            with nc.Block() as block:
                @block.sync
                def _(sp):
                    def load(e, j):
                        sp.dma_start(xg[:, j, :, :], slots_d.rearrange("(e b p) w -> e p b w", p=P, b=BLK)
                                     [bass.ds(e, 1), :, :, :].rearrange("a p b w -> p (a b) w")).then_inc(in4[j], 16)
                        sp.dma_start(wgu[:, j, :, :], io["wgu1"].rearrange("e (k p) n -> e p k n", p=P)
                                     [bass.ds(e, 1), :, :, :].rearrange("a p k n -> p (a k) n")).then_inc(in4[j], 16)
                        sp.dma_start(wd[:, j, :], io["wd1"][bass.ds(e, 1), :, :].rearrange("a p n -> p (a n)"))\
                          .then_inc(in4[j], 16)
                    for e in range(NB):
                        load(e, e)
                    with sp.Fori(1, E1 // NB) as i:
                        for j in range(NB):
                            e = NB * i + j
                            sp.wait_ge(targets, e - (NB - 1))
                            sp.wait_ge(g_down, e - (NB - 1))
                            load(e, j)

                @block.gpsimd
                def _(pool):
                    def send(e, j):
                        wait_apart(pool, g_y, e + 1, passed_pool)
                        for b in range(BLK):
                            pool.indirect_dma_start(
                                y_d, bass.IndirectOffsetOnAxis(ap=target[:, j % NY, b:b + 1], axis=0),
                                y[:, j % NY, b, :], None, bounds_check=T * K1 - 1, oob_is_err=False)\
                                .then_inc(sent4[j % NY], 16)
                    with pool.Fori(0, E1 // NB) as i:
                        for j in range(NB):
                            send(NB * i + j, j)
                    for j in range(NY):
                        pool.wait_ge(sent4[j], 16 * BLK * (E1 // NY))

                @block.scalar
                def _(act):
                    def step(s, j, transposed, hidden, output):
                        if hidden:
                            act.wait_ge(g_mm, s)
                            want(act, g_hid, s - 2)
                            act.activation(sgE[:, (j + 1) % 2, :], bank[:, 2 + (j + 1) % 2, 0:CAP], ACT.Silu)\
                               .then_inc(g_silu, 1)
                        if transposed:
                            act.wait_ge(g_T, s + 1)
                            want(act, g_mm, s - 1)
                            act.activation(xgT[:, j % 2, :, :].rearrange("p k t -> p (k t)"), bank[:, j % 2, :],
                                           ACT.Copy).then_inc(g_xT, 1)

                    experts_pipelined(act, step)

                @block.vector
                def _(dve):
                    def step(s, j, transposed, hidden, output):
                        if transposed:
                            dve.wait_ge(in4[j], 48 * (s // NB) + 64)
                            want(dve, sent4[j % NY], 16 * BLK * (s // NY))
                            dve.tensor_copy(target[:, j % NY, :], xg[:, j, :, D:D + 1].bitcast(I32)
                                            .rearrange("p b a -> p (b a)")).then_inc(targets, 1)
                        if hidden:
                            dve.wait_ge(g_silu, s)
                            want(dve, g_down, s - 2)
                            dve.tensor_tensor(hidT[:, (j + 1) % 2, :], sgE[:, (j + 1) % 2, :],
                                              bank[:, 2 + (j + 1) % 2, CAP:2 * CAP], ALU.mult).then_inc(g_hid, 1)
                        if output:
                            m = (j - 2) % NY
                            dve.wait_ge(g_down, s - 1)
                            want(dve, sent4[m], 16 * BLK * ((s - 2) // NY))
                            dve.tensor_copy(y[:, m, :, :].rearrange("p b n -> p (b n)"), bank[:, 4 + j % 2, :])\
                               .then_inc(g_y, 1)

                    experts_pipelined(dve, step)

                @block.tensor
                def _(pe):
                    def step(s, j, transposed, hidden, output):
                        if transposed:
                            pe.wait_ge(in4[j], 48 * (s // NB) + 64)
                            pe.wait_ge(targets, s + 1)
                            want(pe, g_xT, s - 1)
                            for b in range(BLK):
                                for k in range(KD):
                                    last = pe.transpose(bank[:, j % 2, k * CAP + b * P:k * CAP + (b + 1) * P],
                                                        xg[:, j, b, k * P:(k + 1) * P], ident[:])
                            last.then_inc(g_T, 1)
                        if hidden:
                            q, m = (j + 1) % 2, (j + NB - 1) % NB
                            pe.wait_ge(g_xT, s)
                            want(pe, g_hid, s - 2)
                            for half in range(2):
                                for k in range(KD):
                                    last = pe.matmul(bank[:, 2 + q, half * CAP:(half + 1) * CAP],
                                                     wgu[:, m, k, half * P:(half + 1) * P], xgT[:, q, k, :],
                                                     start=k == 0, stop=k == KD - 1)
                            last.then_inc(g_mm, 1)
                        if output:
                            q, m = j % 2, (j - 2) % NB
                            pe.wait_ge(g_hid, s - 1)
                            want(pe, g_y, s - 3)
                            for b in range(BLK):
                                last = pe.matmul(bank[:, 4 + q, b * D:(b + 1) * D], hidT[:, q, b * P:(b + 1) * P],
                                                 wd[:, m, :], start=True, stop=True)
                            last.then_inc(g_down, 1)

                    experts_pipelined(pe, step)

        five = ExitStack()
        with five:
            yk = sb("choice_rows", [P, 3, CT, K1, D], at=five)
            yk_in = [sem(f"yk_in{i}") for i in range(3)]
            summed, done_out, d5 = sem("summed"), sem("done_out"), sem("dve_steps_5")
            with nc.Block() as block:
                @block.sync
                def _(sp):
                    for c in range(CHUNKS):
                        want(sp, summed, CT * (c - 2))
                        sp.dma_start(yk[:, c % 3, :, :, :], y_d.rearrange("(n p k) d -> p n k d", p=P, k=K1)
                                     [:, c * CT:(c + 1) * CT, :, :]).then_inc(yk_in[c % 3], 16)
                    sp.wait_ge(done_out, 16 * CHUNKS)

                @block.scalar
                def _(act):
                    for c in range(CHUNKS):
                        act.wait_ge(summed, CT * (c + 1))
                        act.dma_start(out_v[:, c * CT:(c + 1) * CT, :], x[:, c * CT:(c + 1) * CT, :]).then_inc(done_out, 16)

                @block.vector
                def _(dve):
                    step = Chain(dve, d5, passed)
                    for c in range(CHUNKS):
                        dve.wait_ge(yk_in[c % 3], 16 * (c // 3 + 1))
                        for k in range(K1):
                            for t in range(CT):
                                row = x[:, c * CT + t, :]
                                last = dve.scalar_tensor_tensor(row, yk[:, c % 3, t, k, :], wk[:, c * CT + t, k:k + 1], row,
                                                                ALU.mult, ALU.add)
                                if k == K1 - 1:
                                    last.then_inc(summed, 1)
                            if k < K1 - 1:
                                step(last)



def hilbert_table():
    f = np.arange(L)
    weight = np.where((f == 0) | (f == L // 2), 1.0, 2.0)[:L // 2 + 1]
    angle = 2 * np.pi / L
    full = np.cos(angle * (np.outer(np.arange(L), f[:L // 2 + 1]) % L)) * weight
    table = full @ np.sin(angle * (np.outer(f[:L // 2 + 1], np.arange(CHUNK)) % L))
    return (table / (2 * L * D)).astype(np.float32)


def kernel(**inputs):
    import concourse.bacc as bacc
    from concourse.bass_utils import run_bass_kernel_spmd

    a = {k: np.asarray(v) for k, v in inputs.items()}
    flip = a["ctx_1024"][:, ::-1, :]
    gu = a["L0_ffn_gate_up_proj"].transpose(2, 0, 1)
    sg = a["L0_ffn_shared_gate_w"].T.reshape(D, 4, 1, P)
    su = a["L0_ffn_shared_up_w"].T.reshape(D, 4, 1, P)
    arrays = {
        "x": a["x"].reshape(T, D),
        "ctxT": flip.reshape(BS, D).T,
        "mask": a["mask_BxS2_bk0"][:, ::-1],
        "g_xattn": a["g_xattn"], "g_ffn": a["g_ffn"],
        "wk0": a["L0_xattn_Wk"], "wqT0": a["L0_xattn_Wq"].T, "wv0": a["L0_xattn_Wv"], "wo0": a["L0_xattn_Wo"],
        "bias0": np.stack([a["L0_xattn_bq"], a["L0_xattn_bk"], a["L0_xattn_bv"]]).reshape(3, KD, P)
                   .transpose(2, 0, 1).reshape(P, 3 * KD),
        "bo0": a["L0_xattn_bo"],
        "htab": hilbert_table(),
        "wgu0": np.concatenate([gu.reshape(D, E0 * 2 * P),
                                np.concatenate([sg, su], 2).reshape(D, 4 * 2 * P)], 1),
        "wd0": np.concatenate([a["L0_ffn_down_proj"].transpose(0, 2, 1).reshape(E0 * P, D),
                               a["L0_ffn_shared_down_w"].T], 0),
        "wr0": np.concatenate([a["L0_ffn_router_weight"]] + 2 * [a["L0_ffn_shared_expert_gate_w"]], 0).T,
        "wk1": a["L1_xattn_W_K"], "wv1": a["L1_xattn_W_V"], "wqT1": a["L1_xattn_W_Q"].T, "wo1": a["L1_xattn_W_O"],
        "wr1": a["L1_ffn_gate_w"].T,
        "wgu1": a["L1_ffn_w_gate_up"], "wd1": a["L1_ffn_w_down"],
        "sgu1": a["L1_ffn_shared_w_gate_up"], "sd1": a["L1_ffn_shared_w_down"],
    }
    arrays = {k: np.ascontiguousarray(v) for k, v in arrays.items()}
    nc = bacc.Bacc("TRN2", target_bir_lowering=False, num_devices=1)
    io = {k: nc.dram_tensor(f"in_{k}", v.shape, mybir.dt.from_np(v.dtype), kind="ExternalInput").ap()
          for k, v in arrays.items()}
    io["out"] = nc.dram_tensor("result", (T, D), F32, kind="ExternalOutput").ap()
    build(nc, io)
    r = run_bass_kernel_spmd(nc, [{f"in_{k}": v for k, v in arrays.items()}], core_ids=[0])
    return r.results[0]["result"].reshape(B, L, D)
```
